# Optimizing a Trainium2 kernel written in Bass

```python
import numpy as np
import jax
import jax.numpy as jnp

def _softmax(x, axis=-1):
    return jax.nn.softmax(x, axis=axis)

def _gelu(x):
    return jax.nn.gelu(x, approximate=True)

def _silu(x):
    return jax.nn.silu(x)

def _sigmoid(x):
    return jax.nn.sigmoid(x)

def _layernorm(x, axis=-1, eps=1e-05):
    m = jnp.mean(x, axis=axis, keepdims=True)
    v = jnp.var(x, axis=axis, keepdims=True)
    return (x - m) / jnp.sqrt(v + eps)

def _scatter_add(tgt, idx, src, axis=0):
    return tgt.at[idx].add(src)

def _segment_sum(src, seg, n):
    return jax.ops.segment_sum(src, seg, n)
kernel_name = 'mk_xattn_ffn_d1_seqx_r8_ffca9c'

def setup_inputs(seed: int=0):
    np.random.seed(seed)
    _w = jnp.asarray

    def _rec_inputs():
        import jax
        import jax.numpy as jnp
        _rk = jax.random.key(seed)
        x = -0.0002928 + 1 * jax.random.normal(jax.random.fold_in(_rk, 1), (128, 64, 128), jnp.float32)
        _lenS = 64 - jax.random.randint(jax.random.fold_in(_rk, 7), (128,), 0, max(1, 64 // 4) + 1, jnp.int32)
        _lenS2 = 64 - jax.random.randint(jax.random.fold_in(_rk, 8), (128,), 0, max(1, 64 // 4) + 1, jnp.int32)
        _ctx_1024P = jax.random.normal(jax.random.fold_in(_rk, 11), (128, 16, 128), jnp.float32)
        _ctx_1024c = jax.random.dirichlet(jax.random.fold_in(_rk, 511), 0.3 * jnp.ones((16,), jnp.float32), (128, 64))
        _ctx_1024t = jnp.einsum('bsk,bkd->bsd', _ctx_1024c, _ctx_1024P)
        _ctx_1024t = _ctx_1024t * jax.lax.rsqrt(jnp.mean(jnp.square(_ctx_1024t)) + 1e-12) * 0.953939
        ctx_1024 = -1.39393e-06 + 0.999914 * (_ctx_1024t + 0.3 * jax.random.normal(jax.random.fold_in(_rk, 611), (128, 64, 128), jnp.float32))
        return (x, ctx_1024)
    x, ctx_1024 = _rec_inputs()

    def _L0_xattn_setup():
        import jax, jax.numpy as jnp
        import numpy as np
        B, S, D, H = (2, 256, 128, 16)
        HD = D // H
        SCALE = HD ** (-0.5)
        NEG = -1000000000.0
        key = jax.random.key(seed)
        ks = jax.random.split(key, 7)
        w_std = 1.0 / np.sqrt(D)
        return {'query': jax.random.normal(ks[0], (B, S, D), dtype=jnp.float32), 'key': jax.random.normal(ks[1], (B, S, D), dtype=jnp.float32), 'value': jax.random.normal(ks[2], (B, S, D), dtype=jnp.float32), 'Wq': jax.random.normal(ks[3], (D, D), dtype=jnp.float32) * w_std, 'Wk': jax.random.normal(ks[4], (D, D), dtype=jnp.float32) * w_std, 'Wv': jax.random.normal(ks[5], (D, D), dtype=jnp.float32) * w_std, 'Wo': jax.random.normal(ks[6], (D, D), dtype=jnp.float32) * w_std}
    _L0_xattn_all = _L0_xattn_setup()
    _L0_xattn_in = {k: v for k, v in _L0_xattn_all.items() if k in ('Wq', 'Wk', 'Wv', 'Wo')}
    del _L0_xattn_all

    def _L0_ffn_setup():
        import jax, jax.numpy as jnp
        import numpy as np
        B, S, D, F, E, TOP_K = (4, 256, 128, 512, 8, 2)
        LN_EPS = 1e-05
        key = jax.random.key(seed)
        ks = jax.random.split(key, 4)
        sc = lambda fan_in: 1.0 / np.sqrt(fan_in)
        return {'x': jax.random.normal(ks[0], (B, S, D), jnp.float32), 'W1': jax.random.normal(ks[1], (E, D, F), jnp.float32) * sc(D), 'b1': jnp.zeros((E, F), jnp.float32), 'W2': jax.random.normal(ks[2], (E, F, D), jnp.float32) * sc(F), 'b2': jnp.zeros((E, D), jnp.float32), 'Wr': jax.random.normal(ks[3], (D, E), jnp.float32) * sc(D), 'br': jnp.zeros((E,), jnp.float32), 'gamma': jnp.ones((D,), jnp.float32), 'beta': jnp.zeros((D,), jnp.float32)}
    _L0_ffn_all = _L0_ffn_setup()
    _L0_ffn_in = {k: v for k, v in _L0_ffn_all.items() if k in ('W1', 'b1', 'W2', 'b2', 'Wr', 'br', 'gamma', 'beta')}
    del _L0_ffn_all
    return {'x': x, 'ctx_1024': ctx_1024, 'L0_xattn_Wq': _L0_xattn_in['Wq'], 'L0_xattn_Wk': _L0_xattn_in['Wk'], 'L0_xattn_Wv': _L0_xattn_in['Wv'], 'L0_xattn_Wo': _L0_xattn_in['Wo'], 'L0_ffn_W1': _L0_ffn_in['W1'], 'L0_ffn_b1': _L0_ffn_in['b1'], 'L0_ffn_W2': _L0_ffn_in['W2'], 'L0_ffn_b2': _L0_ffn_in['b2'], 'L0_ffn_Wr': _L0_ffn_in['Wr'], 'L0_ffn_br': _L0_ffn_in['br'], 'L0_ffn_gamma': _L0_ffn_in['gamma'], 'L0_ffn_beta': _L0_ffn_in['beta']}

def reference(x, ctx_1024, L0_xattn_Wq, L0_xattn_Wk, L0_xattn_Wv, L0_xattn_Wo, L0_ffn_W1, L0_ffn_b1, L0_ffn_W2, L0_ffn_b2, L0_ffn_Wr, L0_ffn_br, L0_ffn_gamma, L0_ffn_beta):
    import jax
    import jax.numpy as jnp

    def _L0_xattn_ref(query, key, value, Wq, Wk, Wv, Wo):
        import jax, jax.numpy as jnp
        import numpy as np
        B, S, D, H = (2, 256, 128, 16)
        HD = D // H
        SCALE = HD ** (-0.5)
        NEG = -1000000000.0
        b, sq, d = query.shape
        sk = key.shape[1]
        q = (query @ Wq.T).reshape(b, sq, H, HD).transpose(0, 2, 1, 3)
        k = (key @ Wk.T).reshape(b, sk, H, HD).transpose(0, 2, 1, 3)
        v = (value @ Wv.T).reshape(b, sk, H, HD).transpose(0, 2, 1, 3)
        scores = jnp.einsum('bhqd,bhkd->bhqk', q, k) * SCALE
        causal = jnp.arange(sq)[:, None] >= jnp.arange(sk)[None, :]
        scores = jnp.where(causal[None, None], scores, NEG)
        attn = jax.nn.softmax(scores, axis=-1)
        out = jnp.einsum('bhqk,bhkd->bhqd', attn, v)
        out = out.transpose(0, 2, 1, 3).reshape(b, sq, d)
        return out @ Wo.T

    def _L0_ffn_ref(x, W1, b1, W2, b2, Wr, br, gamma, beta):
        import jax, jax.numpy as jnp
        import numpy as np
        B, S, D, F, E, TOP_K = (4, 256, 128, 512, 8, 2)
        LN_EPS = 1e-05
        b, s, d = x.shape
        e = Wr.shape[1]
        rw = jax.nn.softmax(x.mean(axis=1) @ Wr + br, axis=-1)
        x_flat = x.reshape(-1, d)
        rw_tok = jnp.repeat(rw, s, axis=0)
        tk_w, tk_i = jax.lax.top_k(rw_tok, TOP_K)
        tk_w = jax.nn.softmax(tk_w, axis=-1)
        h = jax.nn.gelu(jnp.einsum('nd,edf->enf', x_flat, W1) + b1[:, None, :], approximate=False)
        expert_out = jnp.einsum('enf,efd->end', h, W2) + b2[:, None, :]
        onehot = jax.nn.one_hot(tk_i, e, dtype=x.dtype)
        cw = jnp.einsum('nk,nke->ne', tk_w, onehot)
        out = jnp.einsum('ne,end->nd', cw, expert_out).reshape(b, s, d)
        y = out + x
        mu = y.mean(axis=-1, keepdims=True)
        var = y.var(axis=-1, keepdims=True)
        return (y - mu) / jnp.sqrt(var + LN_EPS) * gamma + beta
    x = x + _L0_xattn_ref(_layernorm(x, axis=-1), ctx_1024, ctx_1024, L0_xattn_Wq, L0_xattn_Wk, L0_xattn_Wv, L0_xattn_Wo)
    x = x + _L0_ffn_ref(_layernorm(x, axis=-1), L0_ffn_W1, L0_ffn_b1, L0_ffn_W2, L0_ffn_b2, L0_ffn_Wr, L0_ffn_br, L0_ffn_gamma, L0_ffn_beta)
    return x

_drawn_inputs = setup_inputs


def setup_inputs(seed=0):
    import zlib

    import numpy as np

    out = dict(_drawn_inputs(seed))
    spreads = {'L0_ffn_b1': (0.0, 0.372),
     'L0_ffn_b2': (0.0, 0.273),
     'L0_ffn_br': (0.0, 0.1),
     'L0_ffn_gamma': (1.0, 0.2),
     'L0_ffn_beta': (0.0, 0.1)}
    factors = {}
    for name, (base, spread) in spreads.items():
        noise = np.random.default_rng([zlib.crc32(name.encode()), seed]).standard_normal(out[name].shape)
        drawn = base * np.exp(spread * noise) if base else spread * noise
        out[name] = jnp.asarray(drawn.astype(out[name].dtype))
    for name, factor in factors.items():
        out[name] = (out[name] * factor).astype(out[name].dtype)
    return out
```

```python
from contextlib import ExitStack

import numpy as np

import concourse.bass as bass
from concourse import mybir

F32 = mybir.dt.float32
F32R = mybir.dt.float32r
BF16 = mybir.dt.bfloat16
I32 = mybir.dt.int32
ALU = mybir.AluOpType
ACT = mybir.ActivationFunctionType
AX = mybir.AxisListType

NB, S, D = 128, 64, 128
H, HD = 16, 8
E, F = 8, 512
FC = F // 128
SCALE = HD ** -0.5
EPS = 1e-5
MASKED = -1e30
NT = NB // 2
NP = NT // 2
GB = 8
HALF = GB // 2 * S
MAXBLK = (2 * NB + (GB - 1) * E) // GB
SLOTS = MAXBLK * GB
NOBATCH = NB


def ge(eng, sem, n):
    if isinstance(n, int) and n <= 0:
        return
    eng.wait_ge(sem, n)


LOGIT, EXPW, PROB, TIE, CAND, PICK1, REST, PICK2, CWR, SEL, POS, SLOT = range(12)


def settle(eng, sem):
    eng.wait_ge(sem, 1)


def build(nc, x, ctxT, wq, wk, wv, wo, w1, b1, w2, b2, wr, br, gamma, beta, out):
    es = ExitStack()
    with es:
        def sb(name, shape, dt=F32):
            return es.enter_context(nc.sbuf_tensor(name, shape, dt))

        def sem(name):
            return es.enter_context(nc.semaphore(name))

        X = sb("x_res", [128, NT, D])
        ZT = sb("zT", [128, (NB + 1) * S])
        YT = sb("yT", [128, (NB + 1) * S])
        W1R = sb("w1_raw", [128, 2, F])
        W2R = sb("w2_raw", [128, 2, F])
        B1A = sb("b1_all", [128, E + 1, FC])
        B2A = sb("b2_all", [E, D])
        WR = sb("wr", [128, E])
        BR = sb("br", [128, E])
        GAM = sb("gamma_bc", [128, D])
        BET = sb("beta_bc", [128, D])
        WQ = sb("wq", [128, D])
        WK = sb("wk", [128, D])
        WV = sb("wv", [128, 2, D // 2])
        WO = sb("wo", [128, D])
        WOZ = sb("wo_half", [128, 2, D])
        ident = sb("ident", [128, 128])
        identb = sb("ident_bf", [128, 128], BF16)
        cmask = sb("causal_mask", [128, 8, S], BF16)
        grp8 = sb("group_of_8", [128, 16])
        grp16 = sb("group_of_16", [128, 8])
        jmask = sb("mask_j", [128, 4])
        rmask = sb("mask_r", [128, 4])
        r2mask = sb("mask_r2", [128, 2])
        minus_half = sb("minus_half", [128, 4])
        minus_one = sb("minus_one", [128, 4])
        eps = sb("eps", [128, 4])
        ones = sb("ones", [128, 128])
        before = sb("before", [128, 128])
        iota_e = sb("iota_e", [128, E])
        iota_s = sb("iota_slot", [128, SLOTS])
        IOT = sb("iota_int", [128, SLOTS], I32)
        bcol = sb("batch_minus_filler", [128, 1])
        CT = sb("ctxT_pair", [128, 2, 256])
        XN = sb("xn", [128, 2, D])
        XK = sb("xnT_and_kT", [128, 512])
        QT = sb("qT", [128, 256])
        QR = sb("q_by_row_group", [128, 2, 4, 4, S])
        KM = sb("k_by_head", [128, 2, 4, 4, S])
        VM = sb("v_blocks", [128, 2, 4, 8, 2, HD])
        SS = sb("scores_shifted", [128, 2, 512])
        PP = sb("probs", [128, 4, 512])
        PT = sb("probsT", [128, 2, 512])
        AT = sb("attnT", [128, 2, 2, 128])
        MX = sb("row_max", [128, 2, 8])
        SM = sb("row_sum", [128, 2, 8])
        RC = sb("row_sum_recip", [128, 2, 8])
        ST1 = sb("ln1_stats", [128, 2, 6])
        MV1 = sb("ln1_mv", [128, 2, 2])
        RS1 = sb("ln1_rstd", [128, 2])
        ST2 = sb("ln2_stats", [128, 2, 6])
        MV2 = sb("ln2_mv", [128, 4, 2])
        RS2 = sb("ln2_rstd", [128, 2])
        ZZ = sb("z_pair", [128, 2, D])
        ZS = sb("z_sums", [128, NB])
        RL = sb("router", [128, 12, E])
        RV = sb("router_cols", [128, 16])
        CWT = sb("combine_T", [E, 128])
        B2C = sb("b2_combined", [128, NB])
        NE1 = sb("expert_counts", [E, 4])
        NEI = sb("expert_counts_int", [E, 2], I32)
        NEB = sb("expert_blocks_bc", [E, 128])
        STI = sb("block_starts_int", [128, E + 1], I32)
        IDX = sb("slot_batch_int", [1, SLOTS], I32)
        OH = sb("slot_onehot", [128, 2, SLOTS])
        CW = sb("slot_weight", [128, SLOTS])
        XGH = sb("gather_hi", [128, 2, HALF], F32R)
        XGL = sb("gather_lo", [128, 2, HALF], F32R)
        W1H = sb("w1_hi", [128, 2, F], F32R)
        W1L = sb("w1_lo", [128, 2, F], F32R)
        W2H = sb("w2_hi", [128, 2, F], F32R)
        W2L = sb("w2_lo", [128, 2, F], F32R)
        B1E = sb("b1_expert", [128, 2, FC])
        G = QR[:, :, :, :, :].rearrange("p a b c d -> p (a b c d)").rearrange("p (h c t) -> p h c t", h=2, c=FC)
        GH = sb("gelu_hi", [128, 2, FC, HALF], F32R)
        GL = sb("gelu_lo", [128, 2, FC, HALF], F32R)
        ST3 = sb("ln3_stats", [128, 4, 4, 6])
        MV3 = sb("ln3_mv", [128, 4, 4, 2])
        RS3 = sb("ln3_rstd", [128, 4, 4])
        NB3 = sb("ln3_shift", [128, 4, 4])
        YN = KM[:, :, :, :, :].rearrange("p a b c d -> p (a b c d)").rearrange("p (k m d) -> p k m d", k=4, m=4)

        bank = [es.enter_context(nc.psum_tensor(f"bank{n}", [128, 512], F32)) for n in range(8)]
        S_ps, T_ps, A_ps, J0, J1 = bank[0:2], bank[2:4], bank[4:6], bank[6], bank[7]

        d_w, d_x, d_late = sem("d_weights"), sem("d_x"), sem("d_late")
        d_out = [sem(f"d_out{k}") for k in range(4)]
        d_ex = [sem("d_experts_even"), sem("d_experts_odd")]
        d_ct = [sem("d_ctx_even"), sem("d_ctx_odd")]
        g_const, g_chain, v_setup, v_chain = sem("g_const"), sem("g_chain"), sem("v_setup"), sem("v_chain")
        p_s, v_max, v_sub, a_exp = sem("p_scores"), sem("v_max"), sem("v_shifted"), sem("a_exp")
        v_sum, v_rcp, g_norm = sem("v_sum"), sem("v_rcp"), sem("g_norm")
        p_t, a_pt, p_pv = sem("p_probsT"), sem("a_probsT"), sem("p_pv")
        a_at, p_w, v_x2, v_bn1, v_mv1, v_bn2, v_mv2 = (sem("a_attnT"), sem("p_wo"), sem("v_x2"), sem("v_bn1"),
                                                       sem("v_mv1"), sem("v_bn2"), sem("v_mv2"))
        g_eps1, g_rs1, v_xn, p_xk, a_xk, p_q, a_q = (sem("g_eps1"), sem("g_rstd1"), sem("v_xn"), sem("p_xk"),
                                                     sem("a_xk"), sem("p_q"), sem("a_q"))
        g_qr, g_km, p_v, a_v = sem("g_qr"), sem("g_km"), sem("p_v"), sem("a_v")
        g_qrb, g_kmb, a_vh, v_xnh, v_zh = sem("g_qr_part"), sem("g_km_part"), sem("a_v_part"), sem("v_xn_part"), sem("v_z_part")
        g_eps2, g_rs2, v_z, p_zt, a_zt, v_zs, g_xb = (sem("g_eps2"), sem("g_rstd2"), sem("v_z"), sem("p_zT"),
                                                      sem("a_zT"), sem("v_zsum"), sem("g_x_plus_beta"))
        p_r, v_r, a_r, v_rt, v_yt = sem("p_route"), sem("v_route"), sem("a_route"), sem("v_top_two"), sem("v_yT")
        g_hi, g_lo = sem("g_gather_hi"), sem("g_gather_lo")
        v_whi, v_w = sem("v_weights_hi"), sem("v_weights_split")
        p_h, a_g, v_gh, v_gl, p_o, v_c = (sem("p_hidden"), sem("a_gelu"), sem("v_gelu_hi"), sem("v_gelu_lo"),
                                          sem("p_ffn_out"), sem("v_combined"))
        p_y, v_bn3, v_mv3, g_eps3, g_rs3, g_nb3 = (sem("p_y"), sem("v_bn3"), sem("v_mv3"), sem("g_eps3"),
                                                   sem("g_rstd3"), sem("g_shift3"))
        g_nb3a = sem("g_shift3_part")
        a_yn, g_gam, v_out = sem("a_y_normed"), sem("g_gamma"), sem("v_out")

        block = es.enter_context(nc.Block())

        def expert_range(eng, e2, par):
            lo = eng.value_load(STI[0:1, bass.ds(2 * e2 + par, 1)], min_val=0, max_val=MAXBLK)
            hi = eng.value_load(STI[0:1, bass.ds(2 * e2 + (par + 1), 1)], min_val=1, max_val=MAXBLK)
            return lo, hi

        @block.sync
        def _(sp):
            xv = x.rearrange("(t p) d -> p t d", p=128)
            sp.dma_start(X[:, 0:4, :], xv[:, 0:4, :]).then_inc(d_x, 16)
            for w_sb, w_dram in ((WQ[:, :], wq), (WK[:, :], wk), (WV[:, :, :], wv), (WO[:, :], wo)):
                sp.dma_start(w_sb, w_dram).then_inc(d_w, 16)
            for p in range(2):
                sp.dma_start(CT[:, p, :], ctxT[:, 256 * p:256 * p + 256]).then_inc(d_ct[p], 16)
            for w_sb, w_dram in ((B1A[:, 0:E, :], b1), (B2A[:, :], b2), (WR[:, :], wr),
                                 (BR[:, :], br.partition_broadcast(128)),
                                 (GAM[:, :], gamma.partition_broadcast(128)),
                                 (BET[:, :], beta.partition_broadcast(128))):
                sp.dma_start(w_sb, w_dram).then_inc(d_late, 16)
            sp.wait_ge(d_x, 16)
            sp.dma_start(X[:, 4:8, :], xv[:, 4:8, :]).then_inc(d_x, 16)
            with sp.Fori(1, NP // 2 - 1) as i:
                sp.wait_ge(d_x, 16 * i + 16)
                sp.dma_start(X[:, bass.ds(i * 4 + 4, 4), :], xv[:, bass.ds(i * 4 + 4, 4), :]).then_inc(d_x, 16)
                for par in range(2):
                    sp.wait_ge(p_v, 2 * i + (par - 1))
                    sp.dma_start(CT[:, par, :], ctxT[:, bass.ds(i * 512 + par * 256, 256)]).then_inc(d_ct[par], 16)
            for par in range(2):
                sp.wait_ge(p_v, NP - 3 + par)
                sp.dma_start(CT[:, par, :], ctxT[:, 256 * (NP - 2 + par):256 * (NP - 1 + par)]).then_inc(d_ct[par], 16)
            for e in range(E + 1):
                if e >= 2:
                    sp.wait_ge(v_w, e - 1)
                sp.dma_start(W1R[:, e % 2, :], w1[e % E]).then_inc(d_ex[e % 2], 16)
                sp.dma_start(W2R[:, e % 2, :].rearrange("p (c d) -> p c d", d=D),
                             w2[e % E].rearrange("(c p) d -> p c d", p=128)).then_inc(d_ex[e % 2], 16)
            for k in range(4):
                sp.nop().then_inc(d_out[k], 16)
            ov = out.rearrange("(t p) d -> p t d", p=128)
            with sp.Fori(0, 4) as o:
                for k in range(4):
                    sp.wait_ge(v_out, o * 4 + (k + 1))
                    sp.dma_start(ov[:, bass.ds(o * 16 + 4 * k, 4), :], YN[:, k, :, :]).then_inc(d_out[k], 16)
            for k in range(4):
                sp.wait_ge(d_out[k], 80)

        @block.tensor
        def _(pe):
            def prep_xk(P, par):
                ge(pe, v_xn, P + 1)
                ge(pe, a_v, P)
                for k in range(2):
                    nc.tensor.transpose(J0[:, 128 * k:128 * k + 128], XN[:, k, :], ident[:, :])
                nc.tensor.matmul(J0[:, 256:512], WK[:, :], CT[:, par, :], start=True, stop=True).then_inc(p_xk, 1)

            def prep_q(P):
                ge(pe, a_xk, P + 1)
                nc.tensor.matmul(J0[:, 0:256], WQ[:, :], XK[:, 0:256], start=True, stop=True).then_inc(p_q, 1)

            def prep_v(P, par):
                ge(pe, a_q, P + 1)
                for b in range(4):
                    for j2 in range(2):
                        mm = nc.tensor.matmul(J0[64 * j2:64 * j2 + 64, 64 * b:64 * b + 64],
                                              CT[:, par, 64 * b:64 * b + 64], WV[:, j2, :], start=True, stop=True)
                mm.then_inc(p_v, 1)

            def scores(i, k):
                U, P, s, par, ps = 8 * i + k, 2 * i + k // 4, k % 4, k // 4 % 2, S_ps[k % 2]
                if s == 0:
                    ge(pe, g_qr, P + 1)
                    ge(pe, g_km, P + 1)
                ge(pe, v_sub, U - 1)
                nc.tensor.matmul(ps[:, :], identb[:, :], cmask[:, :, :].rearrange("p a k -> p (a k)"),
                                 start=True, stop=False, skip_group_check=True)
                for rp in range(2):
                    mm = nc.tensor.matmul(ps[:, 256 * rp:256 * rp + 256],
                                          QR[:, par, s, 2 * rp:2 * rp + 2, :].rearrange("p a k -> p (a k)"),
                                          KM[:, par, s, :, :].rearrange("p a k -> p (a k)"),
                                          start=False, stop=True, skip_group_check=True)
                mm.then_inc(p_s, 1)

            def turn(i, k):
                U = 8 * i + k
                ge(pe, g_norm, U + 1)
                ge(pe, a_pt, U - 1)
                for b in range(4):
                    mm = nc.tensor.transpose(T_ps[k % 2][:, 128 * b:128 * b + 128],
                                             PP[:, k % 4, 128 * b:128 * b + 128], ident[:, :])
                mm.then_inc(p_t, 1)

            def attend(i, k):
                U, P, T, s, par = 8 * i + k, 2 * i + k // 4, 4 * i + k // 2, k % 4, k // 4 % 2
                if s == 0:
                    ge(pe, a_v, P + 1)
                if s % 2 == 0:
                    ge(pe, a_at, T - 1)
                ge(pe, a_pt, U + 1)
                for b in range(4):
                    mm = nc.tensor.matmul(A_ps[k // 2 % 2][32 * b:32 * b + 32, 128 * (k % 2):128 * (k % 2) + 128],
                                          VM[:, par, s, 2 * b:2 * b + 2, :, :].rearrange("p a b c -> p (a b c)"),
                                          PT[:, k % 2, 128 * b:128 * b + 128], start=True, stop=True)
                mm.then_inc(p_pv, 1)

            def project(T, t, z_before):
                ge(pe, a_at, T + 1)
                ge(pe, v_x2, T)
                ge(pe, a_zt, z_before)
                for b in range(2):
                    for r2 in range(2):
                        mm = nc.tensor.matmul(J1[64 * b:64 * b + 64, 0:D], AT[:, t, b, 64 * r2:64 * r2 + 64],
                                              WOZ[:, r2, :], start=(r2 == 0), stop=(r2 == 1))
                mm.then_inc(p_w, 1)

            def turn_z(P, x2_before):
                ge(pe, v_z, P + 1)
                ge(pe, v_x2, x2_before)
                for k in range(2):
                    mm = nc.tensor.transpose(J1[:, 128 * k:128 * k + 128], ZZ[:, k, :], ident[:, :])
                mm.then_inc(p_zt, 1)

            def steps(i):
                static = isinstance(i, int)
                for u in range(8):
                    P, U, s, h = 2 * i + u // 4, 8 * i + u, u % 4, u // 4
                    more = not static or P + 1 < NP
                    if not static or U < NB:
                        scores(i, u)
                    if not static or 0 <= U - 2 < NB:
                        turn(i, u - 2)
                    if not static or 0 <= U - 3 < NB:
                        attend(i, u - 3)
                    if s == 0 and more:
                        pe.wait_ge(d_ct[(h + 1) % 2], 16 * i + 16 * (h + 1))
                        prep_xk(P + 1, (h + 1) % 2)
                    if s == 1 and more:
                        prep_q(P + 1)
                    if s == 2 and more:
                        prep_v(P + 1, (h + 1) % 2)
                    if s in (1, 3) and (not static or 0 <= P - 1 < NP):
                        project(4 * i + (2 * h - 2 + s // 2), s // 2, P - 2 + s // 2)
                    if s == 2 and (not static or 0 <= P - 2 < NP):
                        turn_z(P - 2, 4 * i + 2 * h - 1 if not static else min(2 * P - 1, NT))

            pe.wait_ge(g_const, 1)
            pe.wait_ge(v_setup, 1)
            pe.wait_ge(d_w, 64)
            pe.wait_ge(d_ct[0], 16)
            prep_xk(0, 0)
            prep_q(0)
            prep_v(0, 0)
            steps(0)
            steps(1)
            with pe.Fori(2, NB // 8 - 1) as i:
                steps(i)
            steps(NB // 8 - 1)
            steps(NB // 8)

            pe.wait_ge(d_late, 96)
            pe.wait_ge(v_zs, NP)
            pe.wait_ge(a_v, NP)
            nc.tensor.matmul(J0[:, 0:E], ZS[:, :], WR[:, :], start=True, stop=True).then_inc(p_r, 1)
            pe.wait_ge(v_r, 2)
            pe.wait_ge(a_zt, NP)
            nc.tensor.transpose(J1[0:E, 0:128], RL[:, CWR, :], ident[:, :])
            nc.tensor.matmul(A_ps[0][:, 0:E], before[:, :], RL[:, SEL, :], start=True, stop=True)
            nc.tensor.matmul(A_ps[1][0:E, 0:1], RL[:, SEL, :], ones[:, 0:1], start=True, stop=True).then_inc(p_r, 1)
            pe.wait_ge(v_r, 3)
            nc.tensor.matmul(J0[:, 0:E + 1], NEB[:, :], before[0:E, 0:E + 1], start=True, stop=True)
            nc.tensor.matmul(J1[:, 0:NB], B2A[:, :], CWT[:, :], start=True, stop=True).then_inc(p_r, 1)
            pe.wait_ge(v_r, 4)
            nc.tensor.matmul(J0[0:1, 0:SLOTS], bcol[:, :], OH[:, 0, :], start=True, stop=True)
            nc.tensor.matmul(J1[:, 0:SLOTS], ones[:, :], OH[:, 1, :], start=True, stop=True).then_inc(p_r, 1)

            pe.nop().then_inc(p_h, 8)
            pe.nop().then_inc(p_o, 2)
            pe.wait_ge(v_r, 5)
            with pe.Fori(0, E // 2) as e2:
                for par in range(2):
                    lo, hi = expert_range(pe, e2, par)
                    settle(pe, v_setup)
                    pe.wait_ge(v_w, 2 * e2 + (par + 1))
                    with pe.Fori(lo, hi) as g:
                        for half in range(2):
                            pe.wait_ge(g_lo, 8 * g + (4 * half + 4))
                            for c in range(FC):
                                pe.wait_ge(a_g, 8 * g + (4 * half + c + 1))
                                cols, ps = slice(128 * c, 128 * c + 128), bank[c][:, 0:HALF]
                                nc.tensor.matmul(ps, W1H[:, par, cols], XGH[:, half, :], start=True, stop=False)
                                nc.tensor.matmul(ps, W1H[:, par, cols], XGL[:, half, :], start=False, stop=False)
                                nc.tensor.matmul(ps, W1L[:, par, cols], XGH[:, half, :],
                                                 start=False, stop=True).then_inc(p_h, 1)
                        for half in range(2):
                            pe.wait_ge(v_c, 8 * g + (4 * half + 4))
                            ps = bank[4 + half][:, 0:HALF]
                            for c in range(FC):
                                pe.wait_ge(v_gl, 8 * g + (4 * half + c + 9))
                                cols = slice(128 * c, 128 * c + 128)
                                nc.tensor.matmul(ps, W2H[:, par, cols], GH[:, half, c, :], start=(c == 0), stop=False)
                                nc.tensor.matmul(ps, W2H[:, par, cols], GL[:, half, c, :], start=False, stop=False)
                                mm = nc.tensor.matmul(ps, W2L[:, par, cols], GH[:, half, c, :],
                                                      start=False, stop=(c == FC - 1))
                            mm.then_inc(p_o, 1)

            blocks = pe.value_load(STI[0:1, E:E + 1], min_val=1, max_val=MAXBLK)
            pe.wait_ge(v_c, 8 * blocks + 8)
            for t in range(NT):
                ge(pe, a_yn, t - 7)
                nc.tensor.transpose(bank[t % 8][:, 0:D], YT[:, 128 * t:128 * t + 128], ident[:, :]).then_inc(p_y, 1)

        @block.scalar
        def _(act):
            def prep_v(P, par):
                act.wait_ge(p_v, P + 1)
                ge(act, p_pv, 4 * P - 4)
                for j2 in range(2):
                    rows = slice(64 * j2, 64 * j2 + 64)
                    ins = nc.scalar.activation(VM[rows, par, :, :, j2, :].rearrange("p b g d -> p (b g) d"),
                                               J0[rows, 0:256].rearrange("p (n d) -> p n d", d=HD), ACT.Copy)
                    ins.then_inc(a_vh if j2 == 0 else a_v, 1)

            def prep_xk(P):
                act.wait_ge(p_xk, P + 1)
                ge(act, g_km, P)
                ge(act, p_q, P)
                nc.scalar.activation(XK[:, :], J0[:, :], ACT.Copy).then_inc(a_xk, 1)

            def prep_q(P):
                act.wait_ge(p_q, P + 1)
                ge(act, g_qr, P)
                nc.scalar.activation(QT[:, :], J0[:, 0:256], ACT.Copy).then_inc(a_q, 1)

            def steps(i):
                static = isinstance(i, int)
                for u in range(8):
                    P, U, s, h = 2 * i + u // 4, 8 * i + u, u % 4, u // 4
                    more = not static or P + 1 < NP
                    if not static or 0 <= U - 1 < NB:
                        act.wait_ge(v_sub, U)
                        ge(act, p_t, U - 4)
                        nc.scalar.activation(PP[:, (u - 1) % 4, :], SS[:, (u - 1) % 2, :], ACT.Exp,
                                             scale=SCALE).then_inc(a_exp, 1)
                    if s == 1 and more:
                        prep_xk(P + 1)
                    if s == 2 and more:
                        prep_q(P + 1)
                    if s == 3 and more:
                        prep_v(P + 1, (h + 1) % 2)
                    if s == 3 and (not static or 0 <= P - 2 < NP):
                        act.wait_ge(p_zt, P - 1)
                        nc.scalar.activation(ZT[:, bass.ds((P - 2) * 256, 256)], J1[:, 0:256],
                                             ACT.Copy).then_inc(a_zt, 1)
                    if not static or 0 <= U - 2 < NB:
                        act.wait_ge(p_t, U - 1)
                        ge(act, p_pv, U - 3)
                        nc.scalar.activation(PT[:, (u - 2) % 2, :], T_ps[(u - 2) % 2][:, :],
                                             ACT.Copy).then_inc(a_pt, 1)
                    if u % 2 == 0 and (not static or 0 <= U - 4 < NB):
                        t = (u - 4) // 2 % 2
                        act.wait_ge(p_pv, U - 2)
                        ge(act, p_w, 4 * i + (u // 2 - 3))
                        nc.scalar.activation(AT[:, t, :, :].rearrange("p b q -> p (b q)"),
                                             A_ps[t][:, 0:256], ACT.Copy).then_inc(a_at, 1)

            act.wait_ge(v_setup, 2)
            prep_xk(0)
            prep_q(0)
            prep_v(0, 0)
            steps(0)
            steps(1)
            with act.Fori(2, NB // 8 - 1) as i:
                steps(i)
            steps(NB // 8 - 1)
            steps(NB // 8)

            act.wait_ge(v_r, 1)
            nc.scalar.activation(RL[:, EXPW, :], RL[:, LOGIT, :], ACT.Exp, bias=RV[:, 1:2]).then_inc(a_r, 1)
            act.wait_ge(v_rt, 1)
            nc.scalar.activation(RV[:, 9:10], RV[:, 8:9], ACT.Exp).then_inc(a_r, 1)

            act.nop().then_inc(a_g, 4)
            act.wait_ge(v_r, 5)
            with act.Fori(0, E // 2) as e2:
                for par in range(2):
                    lo, hi = expert_range(act, e2, par)
                    act.wait_ge(v_w, 2 * e2 + (par + 1))
                    with act.Fori(lo, hi) as g:
                        for half in range(2):
                            for c in range(FC):
                                act.wait_ge(p_h, 8 * g + (4 * half + c + 9))
                                act.wait_ge(v_gl, 8 * g + (4 * half + c + 1))
                                nc.scalar.activation(G[:, half, c, :], bank[c][:, 0:HALF], ACT.Gelu,
                                                     bias=B1E[:, par, c:c + 1]).then_inc(a_g, 1)

            with act.Fori(0, 4) as o:
                for k in range(4):
                    act.wait_ge(g_nb3, 4 * o + (k + 1))
                    act.wait_ge(d_out[k], 16 * o + 16)
                    for m in range(4):
                        nc.scalar.activation(YN[:, k, m, :], bank[(4 * k + m) % 8][:, 0:D], ACT.Identity,
                                             bias=NB3[:, k, m:m + 1], scale=RS3[:, k, m:m + 1]).then_inc(a_yn, 1)

        @block.vector
        def _(dve):
            chain = [0]

            def link(ins):
                chain[0] += 1
                ins.then_inc(v_chain, 1)
                dve.wait_ge(v_chain, chain[0])

            def stats1(P):
                n = 2 * P + 2
                if not isinstance(P, int):
                    dve.wait_ge(v_max, n)
                settle(dve, v_setup)
                ge(dve, v_xn, P)
                for k in range(2):
                    nc.vector.bn_stats(ST1[:, k, :], X[:, bass.ds(2 * P + k, 1), :].rearrange("p o d -> p (o d)")
                                       ).then_inc(v_bn1, 1)
                settle(dve, v_setup)
                dve.wait_ge(v_bn1, n)
                for k in range(2):
                    nc.vector.bn_aggr(MV1[:, k, :], ST1[:, k, :]).then_inc(v_mv1, 1)

            def norm1(P):
                dve.wait_ge(g_rs1, P + 1)
                ge(dve, p_xk, P)
                for k in range(2):
                    ins = nc.vector.tensor_scalar(XN[:, k, :],
                                                  X[:, bass.ds(2 * P + k, 1), :].rearrange("p o d -> p (o d)"),
                                                  MV1[:, k, 0:1], RS1[:, k:k + 1], ALU.subtract, ALU.mult)
                    ins.then_inc(v_xnh if k == 0 else v_xn, 1)

            def residual(T, slot, k):
                xt = X[:, bass.ds(T, 1), :].rearrange("p o d -> p (o d)")
                dve.wait_ge(p_w, T + 1)
                nc.vector.tensor_tensor(xt, J1[:, 0:D], xt, ALU.add).then_inc(v_x2, 1)
                settle(dve, v_setup)
                dve.wait_ge(v_x2, T + 1)
                nc.vector.bn_stats(ST2[:, k, :], xt).then_inc(v_bn2, 1)
                settle(dve, v_setup)
                dve.wait_ge(v_bn2, T + 1)
                nc.vector.bn_aggr(MV2[:, slot, :], ST2[:, k, :]).then_inc(v_mv2, 1)

            def norm2(P, h):
                dve.wait_ge(g_rs2, P + 1)
                ge(dve, p_zt, P)
                for k in range(2):
                    ins = nc.vector.tensor_scalar(ZZ[:, k, :],
                                                  X[:, bass.ds(2 * P + k, 1), :].rearrange("p o d -> p (o d)"),
                                                  MV2[:, 2 * h + k, 0:1], RS2[:, k:k + 1], ALU.subtract, ALU.mult)
                    ins.then_inc(v_zh if k == 0 else v_z, 1)

            def zsum(P):
                dve.wait_ge(a_zt, P + 1)
                nc.vector.reduce_sum(ZS[:, bass.ds(4 * P, 4)],
                                     ZT[:, bass.ds(256 * P, 256)].rearrange("p (b q) -> p b q", q=S),
                                     AX.X).then_inc(v_zs, 1)

            def steps(i):
                static = isinstance(i, int)
                for u in range(8):
                    P, U, s, h = 2 * i + u // 4, 8 * i + u, u % 4, u // 4
                    if not static or 0 <= U - 1 < NB:
                        k = (u - 1) % 8
                        dve.wait_ge(a_exp, U)
                        nc.vector.reduce_sum(SM[:, k % 2, :], PP[:, k % 4, :].rearrange("p (n k) -> p n k", k=S),
                                             AX.X).then_inc(v_sum, 1)
                        dve.wait_ge(v_sum, U)
                        ge(dve, g_norm, U - 2)
                        nc.vector.reciprocal(RC[:, k % 2, :], SM[:, k % 2, :]).then_inc(v_rcp, 1)
                    if not static or U < NB:
                        ps = S_ps[u % 2][:, :].rearrange("p (n k) -> p n k", k=S)
                        dve.wait_ge(p_s, U + 1)
                        nc.vector.reduce_max(MX[:, u % 2, :], ps, AX.X).then_inc(v_max, 1)
                        dve.wait_ge(v_max, U + 1)
                        ge(dve, a_exp, U - 1)
                        nc.vector.tensor_tensor(SS[:, u % 2, :].rearrange("p (n k) -> p n k", k=S), ps,
                                                MX[:, u % 2, :].unsqueeze(2).to_broadcast([128, 8, S]),
                                                ALU.subtract).then_inc(v_sub, 1)
                    if s == 0 and (not static or 0 <= P - 2 < NP):
                        residual(4 * i + (2 * h - 3), (2 * h + 1) % 4, 1)
                    if s == 0 and (not static or 0 <= P - 3 < NP):
                        zsum(P - 3)
                    if s == 1 and (not static or P + 2 < NP):
                        dve.wait_ge(d_x, 16 * i + 32)
                        stats1(P + 2)
                    if s == 2 and (not static or 0 <= P - 2 < NP):
                        norm2(P - 2, h)
                    if s == 2 and (not static or 0 <= P - 1 < NP):
                        residual(4 * i + (2 * h - 2), (2 * h - 2) % 4, 0)
                    if s == 3 and (not static or P + 2 < NP):
                        norm1(P + 2)

            dve.wait_ge(g_const, 1)
            link(nc.vector.tensor_reduce(jmask[:, :], grp8[:, :].rearrange("p (r j) -> p j r", j=4), AX.X, ALU.add))
            link(nc.vector.tensor_reduce(rmask[:, :], grp8[:, :].rearrange("p (r j) -> p r j", j=4), AX.X, ALU.add))
            link(nc.vector.tensor_reduce(r2mask[:, :], grp16[:, :].rearrange("p (a b) -> p b a", b=2), AX.X, ALU.add))
            dve.wait_ge(d_w, 64)
            link(nc.vector.tensor_scalar(WOZ[:, 0, :], WO[:, :], r2mask[:, 0:1], None, ALU.mult))
            nc.vector.tensor_scalar(WOZ[:, 1, :], WO[:, :], r2mask[:, 1:2], None, ALU.mult).then_inc(v_setup, 1)
            nc.vector.memset(VM[:, :, :, :, :, :], 0.0).then_inc(v_setup, 1)
            dve.wait_ge(d_x, 16)
            stats1(0)
            norm1(0)
            stats1(1)
            norm1(1)
            steps(0)
            steps(1)
            with dve.Fori(2, NB // 8 - 1) as i:
                steps(i)
            steps(NB // 8 - 1)
            steps(NB // 8)
            zsum(NP - 1)

            def pick(w, onehot, top, least):
                link(nc.vector.reduce_max(RV[:, top:top + 1], RL[:, w, :], AX.X))
                link(nc.vector.tensor_scalar(RL[:, TIE, :], RL[:, w, :], RV[:, top:top + 1], None, ALU.is_equal))
                link(nc.vector.scalar_tensor_tensor(RL[:, CAND, :], RL[:, TIE, :], -float(E), iota_e[:, :],
                                                    ALU.mult, ALU.add))
                link(nc.vector.tensor_reduce(RV[:, least:least + 1], RL[:, CAND, :], AX.X, ALU.min))
                link(nc.vector.tensor_scalar(RL[:, onehot, :], RL[:, CAND, :], RV[:, least:least + 1], None,
                                             ALU.is_equal))

            dve.wait_ge(g_const, 2)
            dve.wait_ge(p_r, 1)
            link(nc.vector.scalar_tensor_tensor(RL[:, LOGIT, :], J0[:, 0:E], 1.0 / S, BR[:, :], ALU.mult, ALU.add))
            link(nc.vector.reduce_max(RV[:, 0:1], RL[:, LOGIT, :], AX.X))
            nc.vector.tensor_scalar(RV[:, 1:2], RV[:, 0:1], -1.0, None, ALU.mult).then_inc(v_r, 1)
            dve.wait_ge(a_r, 1)
            link(nc.vector.reduce_sum(RV[:, 2:3], RL[:, EXPW, :], AX.X))
            link(nc.vector.reciprocal(RV[:, 3:4], RV[:, 2:3]))
            link(nc.vector.tensor_scalar(RL[:, PROB, :], RL[:, EXPW, :], RV[:, 3:4], None, ALU.mult))
            pick(PROB, PICK1, 4, 5)
            link(nc.vector.scalar_tensor_tensor(RL[:, REST, :], RL[:, PICK1, :], -4.0, RL[:, PROB, :],
                                                ALU.mult, ALU.add))
            pick(REST, PICK2, 6, 7)
            nc.vector.tensor_tensor(RV[:, 8:9], RV[:, 6:7], RV[:, 4:5], ALU.subtract).then_inc(v_rt, 1)
            dve.wait_ge(a_r, 2)
            link(nc.vector.tensor_scalar(RV[:, 10:11], RV[:, 9:10], 1.0, None, ALU.add))
            link(nc.vector.reciprocal(RV[:, 11:12], RV[:, 10:11]))
            link(nc.vector.tensor_tensor(RV[:, 12:13], RV[:, 9:10], RV[:, 11:12], ALU.mult))
            link(nc.vector.tensor_scalar(RL[:, TIE, :], RL[:, PICK1, :], RV[:, 11:12], None, ALU.mult))
            link(nc.vector.scalar_tensor_tensor(RL[:, CWR, :], RL[:, PICK2, :], RV[:, 12:13], RL[:, TIE, :],
                                                ALU.mult, ALU.add))
            nc.vector.tensor_tensor(RL[:, SEL, :], RL[:, PICK1, :], RL[:, PICK2, :], ALU.add).then_inc(v_r, 1)
            dve.wait_ge(p_r, 2)
            link(nc.vector.tensor_scalar(NEI[:, 0:1], A_ps[1][0:E, 0:1], float(GB - 1), None, ALU.add))
            link(nc.vector.tensor_scalar(NEI[:, 1:2], NEI[:, 0:1], 3, None, ALU.arith_shift_right))
            link(nc.vector.tensor_scalar(NE1[:, 0:1], NEI[:, 1:2], 1.0, None, ALU.max))
            link(nc.vector.tensor_copy(RL[:, POS, :], A_ps[0][:, 0:E]))
            link(nc.vector.tensor_copy(CWT[:, :], J1[0:E, 0:128]))
            nc.vector.tensor_scalar(NEB[:, :], ones[0:E, :], NE1[:, 0:1], None, ALU.mult).then_inc(v_r, 1)
            dve.wait_ge(p_r, 3)
            link(nc.vector.tensor_copy(STI[:, :], J0[:, 0:E + 1]))
            link(nc.vector.tensor_copy(B2C[:, :], J1[:, 0:NB]))
            link(nc.vector.scalar_tensor_tensor(RL[:, SLOT, :], J0[:, 0:E], float(GB), RL[:, POS, :],
                                                ALU.mult, ALU.add))
            for n, onehot in enumerate((PICK1, PICK2)):
                link(nc.vector.tensor_tensor(RL[:, TIE, :], RL[:, SLOT, :], RL[:, onehot, :], ALU.mult))
                link(nc.vector.reduce_sum(RV[:, 13 + n:14 + n], RL[:, TIE, :], AX.X))
                link(nc.vector.tensor_scalar(OH[:, n, :], iota_s[:, :], RV[:, 13 + n:14 + n], None, ALU.is_equal))
            link(nc.vector.tensor_scalar(CW[:, :], OH[:, 0, :], RV[:, 11:12], None, ALU.mult))
            link(nc.vector.tensor_tensor(OH[:, 0, :], OH[:, 0, :], OH[:, 1, :], ALU.add))
            nc.vector.scalar_tensor_tensor(OH[:, 1, :], OH[:, 1, :], RV[:, 12:13], CW[:, :],
                                           ALU.mult, ALU.add).then_inc(v_r, 1)
            dve.wait_ge(v_r, 4)
            dve.wait_ge(p_r, 4)
            link(nc.vector.tensor_scalar(IDX[:, :], J0[0:1, 0:SLOTS], float(NOBATCH), None, ALU.add))
            nc.vector.tensor_copy(CW[:, :], J1[:, 0:SLOTS]).then_inc(v_r, 1)

            dve.nop().then_inc(v_gl, 8)
            dve.nop().then_inc(v_c, 8)

            def split(e, loads, par):
                w1e, w2e = W1R[:, par, :], W2R[:, par, :]
                dve.wait_ge(d_ex[par], 32 * loads)
                nc.vector.tensor_copy(B1E[:, par, :], B1A[:, bass.ds(e, 1), :].rearrange("p o c -> p (o c)")
                                      ).then_inc(v_whi, 1)
                nc.vector.tensor_copy(W1H[:, par, :], w1e).then_inc(v_whi, 1)
                nc.vector.tensor_copy(W2H[:, par, :], w2e).then_inc(v_whi, 1)
                dve.wait_ge(v_whi, 4 * e + 3)
                nc.vector.tensor_tensor(W1L[:, par, :], w1e, W1H[:, par, :], ALU.subtract).then_inc(v_whi, 1)
                dve.wait_ge(v_whi, 4 * e + 4)
                nc.vector.tensor_tensor(W2L[:, par, :], w2e, W2H[:, par, :], ALU.subtract).then_inc(v_w, 1)

            dve.wait_ge(g_const, 3)
            split(0, 1, 0)
            nc.vector.memset(YT[:, NB * S:], 0.0).then_inc(v_yt, 1)
            nc.vector.tensor_tensor(YT[:, 0:NB * S].rearrange("p (b q) -> p b q", q=S),
                                    ZT[:, 0:NB * S].rearrange("p (b q) -> p b q", q=S),
                                    B2C[:, :].unsqueeze(2).to_broadcast([128, NB, S]), ALU.add).then_inc(v_yt, 1)
            dve.wait_ge(v_yt, 2)
            with dve.Fori(0, E // 2) as e2:
                for par in range(2):
                    lo, hi = expert_range(dve, e2, par)
                    split(2 * e2 + (par + 1), e2 + (par + 1), 1 - par)
                    with dve.Fori(lo, hi) as g:
                        for half in range(2):
                            dve.wait_ge(p_o, 2 * g + (half + 1))
                            for c in range(FC):
                                dve.wait_ge(a_g, 8 * g + (4 * half + c + 5))
                                nc.vector.tensor_copy(GH[:, half, c, :], G[:, half, c, :]).then_inc(v_gh, 1)
                                dve.wait_ge(v_gh, 8 * g + (4 * half + c + 1))
                                nc.vector.tensor_tensor(GL[:, half, c, :], G[:, half, c, :], GH[:, half, c, :],
                                                        ALU.subtract).then_inc(v_gl, 1)
                        for half in range(2):
                            dve.wait_ge(p_o, 2 * g + (half + 3))
                            for k in range(4):
                                b = dve.value_load(IDX[0:1, bass.ds(8 * g + (4 * half + k), 1)], min_val=0, max_val=NB)
                                yt = YT[:, bass.ds(b * S, S)]
                                dve.wait_ge(v_c, 8 * g + (4 * half + k + 8))
                                nc.vector.scalar_tensor_tensor(
                                    yt, bank[4 + half][:, S * k:S * k + S], CW[:, bass.ds(8 * g + (4 * half + k), 1)],
                                    yt, ALU.mult, ALU.add).then_inc(v_c, 1)

            def stats3(o, k):
                for m in range(4):
                    settle(dve, v_setup)
                    dve.wait_ge(p_y, 16 * o + (4 * k + m + 1))
                    nc.vector.bn_stats(ST3[:, k, m, :], bank[(4 * k + m) % 8][:, 0:D]).then_inc(v_bn3, 1)
                for m in range(4):
                    settle(dve, v_setup)
                    dve.wait_ge(v_bn3, 16 * o + (4 * k + m + 1))
                    nc.vector.bn_aggr(MV3[:, k, m, :], ST3[:, k, m, :]).then_inc(v_mv3, 1)

            def finish(o, k, T):
                dve.wait_ge(g_gam, 4 * o + (k + 1))
                nc.vector.tensor_tensor(YN[:, k, :, :], YN[:, k, :, :], X[:, bass.ds(T, 4), :],
                                        ALU.add).then_inc(v_out, 1)

            dve.wait_ge(g_xb, NP)
            stats3(0, 0)
            for k in range(1, 4):
                stats3(0, k)
                finish(0, k - 1, 4 * k - 4)
            with dve.Fori(1, 4) as o:
                for k in range(4):
                    stats3(o, k)
                    if k == 0:
                        dve.wait_ge(g_gam, 4 * o)
                        nc.vector.tensor_tensor(YN[:, 3, :, :], YN[:, 3, :, :], X[:, bass.ds(16 * o - 4, 4), :],
                                                ALU.add).then_inc(v_out, 1)
                    else:
                        finish(o, k - 1, 16 * o + (4 * k - 4))
            finish(3, 3, 60)

        @block.gpsimd
        def _(pool):
            chain = [0]

            def link(ins):
                chain[0] += 1
                ins.then_inc(g_chain, 1)
                pool.wait_ge(g_chain, chain[0])

            def keep(t, op, base, pattern, mult, fill=0.0):
                link(nc.gpsimd.affine_select(out=t, in_=t, compare_op=op, fill=fill, base=base, pattern=pattern,
                                             channel_multiplier=mult))

            for t, v in ((ident[:, :], 0.0), (cmask[:, :, :], 0.0), (grp8[:, :], 1.0), (grp16[:, :], 1.0),
                         (minus_half[:, :], -0.5), (minus_one[:, :], -1.0), (eps[:, :], EPS)):
                link(nc.gpsimd.memset(t, v))
            keep(ident[:, :], ALU.not_equal, 0, [[-1, 128]], 1, 1.0)
            link(nc.gpsimd.tensor_copy(identb[:, :], ident[:, :]))
            for q0 in (0, 64):
                keep(cmask[q0:q0 + 64, :, :], ALU.is_ge, 0, [[0, 8], [-1, S]], 1, MASKED)
            keep(grp8[:, :], ALU.is_ge, 0, [[-8, 16]], 1)
            keep(grp8[:, :], ALU.is_ge, 7, [[8, 16]], -1)
            keep(grp16[:, :], ALU.is_ge, 0, [[-16, 8]], 1)
            keep(grp16[:, :], ALU.is_ge, 15, [[16, 8]], -1)
            pool.nop().then_inc(g_const, 1)

            def rstd(mv, rs, eps_sem, rs_sem, n):
                nc.gpsimd.tensor_tensor(rs, mv, eps[:, 0:rs.shape[-1]], ALU.add).then_inc(eps_sem, 1)
                pool.wait_ge(eps_sem, n)
                nc.gpsimd.tensor_tensor(rs, rs, minus_half[:, 0:rs.shape[-1]], ALU.pow).then_inc(rs_sem, 1)

            def rstd1(P):
                pool.wait_ge(v_mv1, 2 * P + 2)
                rstd(MV1[:, :, 1], RS1[:, :], g_eps1, g_rs1, P + 1)

            def rstd2(P, h):
                pool.wait_ge(v_mv2, 2 * P + 2)
                ge(pool, v_z, P)
                rstd(MV2[:, 2 * h:2 * h + 2, 1], RS2[:, :], g_eps2, g_rs2, P + 1)

            def spread_q(P, par):
                pool.wait_ge(a_q, P + 1)
                ge(pool, p_s, 4 * P - 4)
                for b in range(4):
                    ins = nc.gpsimd.tensor_tensor(QR[:, par, b, :, :],
                                                  QT[:, S * b:S * b + S].unsqueeze(1).to_broadcast([128, 4, S]),
                                                  rmask[:, :].unsqueeze(2).to_broadcast([128, 4, S]), ALU.mult)
                    ins.then_inc(g_qr if b == 3 else g_qrb, 1)

            def spread_k(P, par):
                pool.wait_ge(a_xk, P + 1)
                ge(pool, p_s, 4 * P - 4)
                for b in range(4):
                    ins = nc.gpsimd.tensor_tensor(KM[:, par, b, :, :],
                                                  XK[:, 256 + S * b:256 + S * b + S].unsqueeze(1)
                                                  .to_broadcast([128, 4, S]),
                                                  jmask[:, :].unsqueeze(2).to_broadcast([128, 4, S]), ALU.mult)
                    ins.then_inc(g_km if b == 3 else g_kmb, 1)

            def steps(i):
                static = isinstance(i, int)
                for u in range(8):
                    P, U, s, h = 2 * i + u // 4, 8 * i + u, u % 4, u // 4
                    more = not static or P + 1 < NP
                    if not static or 0 <= U - 1 < NB:
                        k = (u - 1) % 8
                        pp = PP[:, k % 4, :].rearrange("p (n k) -> p n k", k=S)
                        pool.wait_ge(v_rcp, U)
                        nc.gpsimd.tensor_tensor(pp, pp, RC[:, k % 2, :].unsqueeze(2).to_broadcast([128, 8, S]),
                                                ALU.mult).then_inc(g_norm, 1)
                    if s == 1 and (not static or 0 <= P - 2 < NP):
                        rstd2(P - 2, h)
                    if s == 1 and more:
                        spread_k(P + 1, (h + 1) % 2)
                    if s == 2 and (not static or P + 2 < NP):
                        rstd1(P + 2)
                    if s == 2 and more:
                        spread_q(P + 1, (h + 1) % 2)
                    if s == 3 and (not static or 0 <= P - 2 < NP):
                        pool.wait_ge(v_z, P - 1)
                        xp = X[:, bass.ds(4 * i + (2 * h - 4), 2), :]
                        nc.gpsimd.tensor_tensor(xp, xp, BET[:, :].unsqueeze(1).to_broadcast([128, 2, D]),
                                                ALU.add).then_inc(g_xb, 1)

            pool.wait_ge(v_chain, 3)
            rstd1(0)
            rstd1(1)
            spread_k(0, 0)
            spread_q(0, 0)
            link(nc.gpsimd.memset(ones[:, :], 1.0))
            link(nc.gpsimd.memset(before[:, :], 1.0))
            keep(before[:, :], ALU.is_gt, 0, [[1, 128]], -1)
            link(nc.gpsimd.iota(IOT[:, :], pattern=[[1, SLOTS]], base=0, channel_multiplier=0))
            link(nc.gpsimd.tensor_copy(iota_s[:, :], IOT[:, :]))
            link(nc.gpsimd.tensor_copy(iota_e[:, :], IOT[:, 0:E]))
            link(nc.gpsimd.iota(IOT[:, 0:1], pattern=[[0, 1]], base=-NOBATCH, channel_multiplier=1))
            link(nc.gpsimd.tensor_copy(bcol[:, :], IOT[:, 0:1]))
            pool.nop().then_inc(g_const, 1)
            pool.wait_ge(d_late, 96)
            steps(0)
            steps(1)
            with pool.Fori(2, NB // 8 - 1) as i:
                steps(i)
            steps(NB // 8 - 1)
            steps(NB // 8)
            for t in (ZT[:, NB * S:], B1A[:, E, :]):
                link(nc.gpsimd.memset(t, 0.0))
            pool.nop().then_inc(g_const, 1)

            pool.wait_ge(v_r, 5)
            blocks = pool.value_load(STI[0:1, E:E + 1], min_val=1, max_val=MAXBLK)
            with pool.Fori(0, blocks) as g:
                for half in range(2):
                    pool.wait_ge(p_h, 8 * g + (4 * half + 4))
                    src = []
                    for k in range(4):
                        b = pool.value_load(IDX[0:1, bass.ds(8 * g + (4 * half + k), 1)], min_val=0, max_val=NB)
                        src.append(ZT[:, bass.ds(b * S, S)])
                        nc.gpsimd.tensor_copy(XGH[:, half, S * k:S * k + S], src[k]).then_inc(g_hi, 1)
                    for k in range(4):
                        if k == 0:
                            n = pool.snap(8 * g + (4 * half + 4))
                            settle(pool, v_setup)
                            pool.wait_ge(g_hi, n)
                        nc.gpsimd.tensor_tensor(XGL[:, half, S * k:S * k + S], src[k],
                                                XGH[:, half, S * k:S * k + S], ALU.subtract).then_inc(g_lo, 1)

            with pool.Fori(0, 4) as o:
                for k in range(4):
                    pool.wait_ge(v_mv3, 16 * o + (4 * k + 4))
                    rstd(MV3[:, k, :, 1], RS3[:, k, :], g_eps3, g_rs3, 4 * o + (k + 1))
                    pool.wait_ge(g_rs3, 4 * o + (k + 1))
                    nc.gpsimd.tensor_tensor(NB3[:, k, :], MV3[:, k, :, 0], RS3[:, k, :], ALU.mult).then_inc(g_nb3a, 1)
                    pool.wait_ge(g_nb3a, 4 * o + (k + 1))
                    nc.gpsimd.tensor_tensor(NB3[:, k, :], NB3[:, k, :], minus_one[:, :], ALU.mult).then_inc(g_nb3, 1)
                    pool.wait_ge(a_yn, 16 * o + (4 * k + 4))
                    nc.gpsimd.tensor_tensor(YN[:, k, :, :], YN[:, k, :, :],
                                            GAM[:, :].unsqueeze(1).to_broadcast([128, 4, D]),
                                            ALU.mult).then_inc(g_gam, 1)


def kernel(**inputs):
    import concourse.bacc as bacc
    from concourse.bass_utils import run_bass_kernel_spmd

    a = {k: np.asarray(v) for k, v in inputs.items()}
    wvT = a["L0_xattn_Wv"].T.reshape(D, 4, 2, 2, HD)
    wv = wvT.transpose(0, 3, 1, 2, 4)
    wv = wv.reshape(D, 2, 2, 2, 2, HD).transpose(0, 1, 2, 4, 3, 5)
    woT = a["L0_xattn_Wo"].T.reshape(2, 2, 2, 2, HD, D)
    arrays = {
        "x": a["x"].reshape(NB * S, D),
        "ctxT": a["ctx_1024"].reshape(NB * S, D).T,
        "wq": a["L0_xattn_Wq"].T,
        "wk": a["L0_xattn_Wk"].T,
        "wv": wv.reshape(D, 2, D // 2),
        "wo": woT.transpose(0, 2, 1, 3, 4, 5).reshape(D, D),
        "w1": a["L0_ffn_W1"],
        "b1": a["L0_ffn_b1"].reshape(E, FC, 128).transpose(2, 0, 1),
        "w2": a["L0_ffn_W2"],
        "b2": a["L0_ffn_b2"],
        "wr": a["L0_ffn_Wr"],
        "br": a["L0_ffn_br"],
        "gamma": a["L0_ffn_gamma"],
        "beta": a["L0_ffn_beta"],
    }
    arrays = {k: np.ascontiguousarray(v) for k, v in arrays.items()}
    nc = bacc.Bacc("TRN2", target_bir_lowering=False, num_devices=1)
    args = {k: nc.dram_tensor("in_" + k, v.shape, F32, kind="ExternalInput").ap() for k, v in arrays.items()}
    out = nc.dram_tensor("out", (NB * S, D), F32, kind="ExternalOutput").ap()
    build(nc, **args, out=out)
    r = run_bass_kernel_spmd(nc, [{"in_" + k: v for k, v in arrays.items()}], core_ids=[0])
    return r.results[0]["out"].reshape(NB, S, D)
```

```python
from contextlib import ExitStack

import numpy as np

import concourse.bass as bass
from concourse import mybir

F32 = mybir.dt.float32
F32R = mybir.dt.float32r
BF16 = mybir.dt.bfloat16
I32 = mybir.dt.int32
ALU = mybir.AluOpType
ACT = mybir.ActivationFunctionType
AX = mybir.AxisListType

NB, S, D = 128, 64, 128
H, HD = 16, 8
E, F = 8, 512
FC = F // 128
SCALE = HD ** -0.5
EPS = 1e-5
MASKED = -1e30
NT = NB // 2
NP = NT // 2
GB = 8
HALF = GB // 2 * S
MAXBLK = (2 * NB + (GB - 1) * E) // GB
SLOTS = (MAXBLK + 1) * GB
NOBATCH = NB


def ge(eng, sem, n):
    if isinstance(n, int) and n <= 0:
        return
    eng.wait_ge(sem, n)


LOGIT, EXPW, PROB, TIE, CAND, PICK1, REST, PICK2, CWR, SEL, POS, SLOT = range(12)


def settle(eng, sem):
    eng.wait_ge(sem, 1)


def build(nc, x, ctxT, wq, wk, wv, wo, w1, b1, w2, b2, wr, br, gamma, beta, out):
    es = ExitStack()
    with es:
        def sb(name, shape, dt=F32):
            return es.enter_context(nc.sbuf_tensor(name, shape, dt))

        def sem(name):
            return es.enter_context(nc.semaphore(name))

        X = sb("x_res", [128, NT, D])
        ZT = sb("zT", [128, (NB + GB) * S])
        YT = sb("yT", [128, (NB + GB) * S])
        W1R = sb("w1_raw", [128, 2, F])
        W2R = sb("w2_raw", [128, 2, F])
        B1A = sb("b1_all", [128, E + 1, FC])
        B2A = sb("b2_all", [E, D])
        WR = sb("wr", [128, E])
        BR = sb("br", [128, E])
        GAM = sb("gamma_bc", [128, D])
        BET = sb("beta_bc", [128, D])
        WQ = sb("wq", [128, D])
        WK = sb("wk", [128, D])
        WV = sb("wv", [128, 2, D // 2])
        WO = sb("wo", [128, D])
        WOZ = sb("wo_half", [128, 2, D])
        ident = sb("ident", [128, 128])
        identb = sb("ident_bf", [128, 128], BF16)
        cmask = sb("causal_mask", [128, 8, S], BF16)
        grp8 = sb("group_of_8", [128, 16])
        grp16 = sb("group_of_16", [128, 8])
        jmask = sb("mask_j", [128, 4])
        r2mask = sb("mask_r2", [128, 2])
        minus_half = sb("minus_half", [128, 4])
        minus_one = sb("minus_one", [128, 4])
        eps = sb("eps", [128, 4])
        ones = sb("ones", [128, 128])
        before = sb("before", [128, 128])
        iota_e = sb("iota_e", [128, E])
        iota_s = sb("iota_slot", [128, SLOTS])
        iota_f = sb("iota_slot_of_block", [128, SLOTS])
        IOT = sb("iota_int", [128, SLOTS], I32)
        bcol = sb("batch_minus_filler", [128, 2])
        CT = sb("ctxT_pair", [128, 2, 256])
        XN = sb("xn", [128, 2, D])
        XK = sb("xnT_and_kT", [128, 512])
        QR = sb("q_by_row_group", [128, 2, 4, 4, S])
        KM = sb("k_by_head", [128, 2, 4, 4, S])
        VM = sb("v_blocks", [128, 2, 4, 8, 2, HD])
        SS = sb("scores_shifted", [128, 2, 512])
        PP = sb("probs", [128, 4, 512])
        PT = sb("probsT", [128, 2, 512])
        AT = sb("attnT", [128, 2, 2, 128])
        MX = sb("row_max", [128, 2, 8])
        SM = sb("row_sum", [128, 2, 8])
        RC = sb("row_sum_recip", [128, 2, 8])
        ST1 = sb("ln1_stats", [128, 2, 6])
        MV1 = sb("ln1_mv", [128, 2, 2])
        RS1 = sb("ln1_rstd", [128, 2])
        SH1 = sb("ln1_shift", [128, 2])
        ST2 = sb("ln2_stats", [128, 2, 6])
        MV2 = sb("ln2_mv", [128, 4, 2])
        RS2 = sb("ln2_rstd", [128, 2])
        SH2 = sb("ln2_shift", [128, 2])
        ZZ = sb("z_pair", [128, 2, D])
        ZS = sb("z_sums", [128, NB])
        RL = sb("router", [128, 12, E])
        RV = sb("router_cols", [128, 16])
        CWT = sb("combine_T", [E, 128 + 8])
        NE1 = sb("expert_counts", [E, 4])
        NEI = sb("expert_counts_int", [E, 2], I32)
        NEB = sb("expert_blocks_bc", [E, 128])
        STI = sb("block_starts_int", [128, E + 1], I32)
        IDX = sb("slot_batch_int", [1, SLOTS], I32)
        OH = PP[:, 2:4, 0:SLOTS]
        OHF = PP[:, 1, 0:SLOTS]
        CW = sb("slot_weight", [128, SLOTS])
        XR = PP[:, 0:1, :].rearrange("p a (h t) -> p (a h) t", h=2)
        XGH = sb("gather_hi", [128, 2, HALF], F32R)
        XGL = sb("gather_lo", [128, 2, HALF], F32R)
        W1H = sb("w1_hi", [128, 2, F], F32R)
        W1L = sb("w1_lo", [128, 2, F], F32R)
        W2H = sb("w2_hi", [128, 2, F], F32R)
        W2L = sb("w2_lo", [128, 2, F], F32R)
        B1E = sb("b1_expert", [128, 2, FC])
        G = QR[:, :, :, :, :].rearrange("p a b c d -> p (a b c d)").rearrange("p (h c t) -> p h c t", h=2, c=FC)
        GH = sb("gelu_hi", [128, 2, FC, HALF], F32R)
        GL = sb("gelu_lo", [128, 2, FC, HALF], F32R)
        ST3 = sb("ln3_stats", [128, 4, 4, 6])
        MV3 = sb("ln3_mv", [128, 4, 4, 2])
        RS3 = sb("ln3_rstd", [128, 4, 4])
        NB3 = sb("ln3_shift", [128, 4, 4])
        CWX = ZT[0:E, 0:2048].rearrange("p (k t) -> p k t", k=4)
        YN = KM[:, :, :, :, :].rearrange("p a b c d -> p (a b c d)").rearrange("p (k m d) -> p k m d", k=4, m=4)

        bank = [es.enter_context(nc.psum_tensor(f"bank{n}", [128, 512], F32)) for n in range(8)]
        S_ps, T_ps, A_ps, J0, J1 = bank[0:2], bank[2:4], bank[4:6], bank[6], bank[7]

        d_w, d_x, d_late = sem("d_weights"), sem("d_x"), sem("d_late")
        d_out = [sem(f"d_out{k}") for k in range(4)]
        d_ex = [sem("d_experts_even"), sem("d_experts_odd")]
        d_ct = [sem("d_ctx_even"), sem("d_ctx_odd")]
        g_const, g_chain, v_setup, v_chain = sem("g_const"), sem("g_chain"), sem("v_setup"), sem("v_chain")
        p_s, v_max, v_sub, a_exp = sem("p_scores"), sem("v_max"), sem("v_shifted"), sem("a_exp")
        v_sum, v_rcp, g_norm = sem("v_sum"), sem("v_rcp"), sem("g_norm")
        p_t, a_pt, p_pv = sem("p_probsT"), sem("a_probsT"), sem("p_pv")
        a_at, p_w, v_x2, v_bn1, v_mv1, v_bn2, v_mv2 = (sem("a_attnT"), sem("p_wo"), sem("v_x2"), sem("v_bn1"),
                                                       sem("v_mv1"), sem("v_bn2"), sem("v_mv2"))
        g_eps1, g_rs1, v_sh1, a_xn, p_xk, a_xk, p_q, a_q = (sem("g_eps1"), sem("g_rstd1"), sem("v_shift1"),
                                                            sem("a_xn"), sem("p_xk"), sem("a_xk"), sem("p_q"),
                                                            sem("a_q"))
        g_km, p_v, a_v = sem("g_km"), sem("p_v"), sem("a_v")
        a_qp, g_kmb, a_vh, a_xnp, a_zp = (sem("a_q_part"), sem("g_km_part"), sem("a_v_part"), sem("a_xn_part"),
                                          sem("a_z_part"))
        g_eps2, g_rs2, v_sh2, a_z, p_zt, a_zt, v_zs, g_xb = (sem("g_eps2"), sem("g_rstd2"), sem("v_shift2"),
                                                             sem("a_z"), sem("p_zT"), sem("a_zT"), sem("v_zsum"),
                                                             sem("g_x_plus_beta"))
        p_r, v_r, a_r, v_rt, a_yt = sem("p_route"), sem("v_route"), sem("a_route"), sem("v_top_two"), sem("a_yT")
        d_xr = [sem("d_gather_half0"), sem("d_gather_half1")]
        a_hi, g_lo = sem("a_gather_hi"), sem("g_gather_lo")
        a_whi, g_w0, v_w, v_b1 = (sem("a_weights_hi"), sem("g_weights_0_split"), sem("v_weights_split"),
                                  sem("v_b1_expert"))
        v_wl = sem("v_weights_lo_part")
        p_begun = sem("p_expert_begun")
        p_h, a_g, a_gh, v_gh, v_gl, g_gl, p_o, v_c = (sem("p_hidden"), sem("a_gelu"), sem("a_gelu_hi"),
                                                      sem("v_gelu_hi"), sem("v_gelu_lo"), sem("g_gelu_lo"),
                                                      sem("p_ffn_out"), sem("v_combined"))
        p_y, v_bn3, v_mv3, g_eps3, g_rs3, g_nb3 = (sem("p_y"), sem("v_bn3"), sem("v_mv3"), sem("g_eps3"),
                                                   sem("g_rstd3"), sem("g_shift3"))
        g_nb3a = sem("g_shift3_part")
        a_cw = sem("a_token_weights")
        a_yn, g_gam, v_out = sem("a_y_normed"), sem("g_gamma"), sem("v_out")

        block = es.enter_context(nc.Block())

        def load_values(engine, cells, least, most, unchecked=None):
            return nc.values_load_multi_w_load_instructions(cells, engines=(engine,), min_val=least, max_val=most,
                                                            skip_runtime_bounds_check_because=unchecked)[1]

        def expert_bounds(engine, e2):
            return load_values(engine, STI[0:1, bass.ds(2 * e2, 3)], 0, MAXBLK)

        def half_batches(engine, g, half):
            return load_values(engine, IDX[0:1, bass.ds(8 * g + 4 * half, 4)], 0, NB + GB - 1,
                               "a batch or filler by the one-hots")

        def hidden_bank(half, c):
            return bank[c if half == 0 else (4, 5, 0, 1)[c]]

        @block.sync
        def _(sp):
            def load_expert(w1e, w2e, par):
                sp.dma_start(W1R[:, par, :], w1e).then_inc(d_ex[par], 16)
                sp.dma_start(W2R[:, par, :].rearrange("p (c d) -> p c d", d=D),
                             w2e.rearrange("(c p) d -> p c d", p=128)).then_inc(d_ex[par], 16)

            def gather(g):
                for half in range(2):
                    b = half_batches(mybir.EngineType.SP, g, half)
                    sp.wait_ge(g_lo, 2 * g + (half + 1))
                    for k in range(4):
                        sp.dma_start(XR[:, half, S * k:S * k + S],
                                     ZT[:, bass.ds(b[k] * S, S)]).then_inc(d_xr[half], 16)

            def gather_experts(e2, more):
                bounds = expert_bounds(mybir.EngineType.SP, e2)
                for par in range(2):
                    if not more and par == 0:
                        sp.wait_ge(v_w, E - 1)
                        load_expert(w1[0], w2[0], 0)
                    elif more:
                        settle(sp, v_setup)
                        sp.wait_ge(v_w, 2 * e2 + (par + 1))
                        load_expert(w1[bass.ds(2 * e2 + (par + 2), 1)].rearrange("o p f -> (o p) f"),
                                    w2[bass.ds(2 * e2 + (par + 2), 1)].rearrange("o f d -> (o f) d"), par)
                    with sp.Fori(bounds[par], bounds[par + 1]) as g:
                        gather(g)
                return bounds[2]

            xv = x.rearrange("(t p) d -> p t d", p=128)
            sp.dma_start(X[:, 0:4, :], xv[:, 0:4, :]).then_inc(d_x, 16)
            for w_sb, w_dram in ((WQ[:, :], wq), (WK[:, :], wk), (WV[:, :, :], wv), (WO[:, :], wo)):
                sp.dma_start(w_sb, w_dram).then_inc(d_w, 16)
            for p in range(2):
                sp.dma_start(CT[:, p, :], ctxT[:, 256 * p:256 * p + 256]).then_inc(d_ct[p], 16)
            for w_sb, w_dram in ((B1A[:, 0:E, :], b1), (B2A[:, :], b2), (WR[:, :], wr),
                                 (BR[:, :], br.partition_broadcast(128)),
                                 (GAM[:, :], gamma.partition_broadcast(128)),
                                 (BET[:, :], beta.partition_broadcast(128))):
                sp.dma_start(w_sb, w_dram).then_inc(d_late, 16)
            sp.wait_ge(d_x, 16)
            sp.dma_start(X[:, 4:8, :], xv[:, 4:8, :]).then_inc(d_x, 16)
            with sp.Fori(1, NP // 2 - 1) as i:
                sp.wait_ge(d_x, 16 * i + 16)
                sp.dma_start(X[:, bass.ds(i * 4 + 4, 4), :], xv[:, bass.ds(i * 4 + 4, 4), :]).then_inc(d_x, 16)
                for par in range(2):
                    sp.wait_ge(p_v, 2 * i + (par - 1))
                    sp.dma_start(CT[:, par, :], ctxT[:, bass.ds(i * 512 + par * 256, 256)]).then_inc(d_ct[par], 16)
            for par in range(2):
                sp.wait_ge(p_v, NP - 3 + par)
                sp.dma_start(CT[:, par, :], ctxT[:, 256 * (NP - 2 + par):256 * (NP - 1 + par)]).then_inc(d_ct[par], 16)
            for e in range(2):
                load_expert(w1[e], w2[e], e)
            sp.wait_ge(v_r, 5)
            sp.wait_ge(g_w0, 2)
            sp.wait_ge(a_zt, NP)
            with sp.Fori(0, E // 2 - 1) as e2:
                gather_experts(e2, True)
            gather(gather_experts(E // 2 - 1, False))
            for k in range(4):
                sp.nop().then_inc(d_out[k], 16)
            ov = out.rearrange("(t p) d -> p t d", p=128)
            with sp.Fori(0, 4) as o:
                for k in range(4):
                    sp.wait_ge(v_out, o * 4 + (k + 1))
                    sp.dma_start(ov[:, bass.ds(o * 16 + 4 * k, 4), :], YN[:, k, :, :]).then_inc(d_out[k], 16)
            for k in range(4):
                sp.wait_ge(d_out[k], 80)

        @block.tensor
        def _(pe):
            def prep_xk(P, par):
                ge(pe, a_xn, P + 1)
                ge(pe, a_v, P)
                for k in range(2):
                    nc.tensor.transpose(J0[:, 128 * k:128 * k + 128], XN[:, k, :], ident[:, :])
                nc.tensor.matmul(J0[:, 256:512], WK[:, :], CT[:, par, :], start=True, stop=True).then_inc(p_xk, 1)

            def prep_q(P):
                ge(pe, a_xk, P + 1)
                nc.tensor.matmul(J0[:, 0:256], WQ[:, :], XK[:, 0:256], start=True, stop=True).then_inc(p_q, 1)

            def prep_v(P, par):
                ge(pe, a_q, P + 1)
                for b in range(4):
                    for j2 in range(2):
                        mm = nc.tensor.matmul(J0[64 * j2:64 * j2 + 64, 64 * b:64 * b + 64],
                                              CT[:, par, 64 * b:64 * b + 64], WV[:, j2, :], start=True, stop=True)
                mm.then_inc(p_v, 1)

            def scores(i, k):
                U, P, s, par, ps = 8 * i + k, 2 * i + k // 4, k % 4, k // 4 % 2, S_ps[k % 2]
                if s == 0:
                    ge(pe, a_q, P + 1)
                    ge(pe, g_km, P + 1)
                ge(pe, v_sub, U - 1)
                nc.tensor.matmul(ps[:, :], identb[:, :], cmask[:, :, :].rearrange("p a k -> p (a k)"),
                                 start=True, stop=False, skip_group_check=True)
                for rp in range(2):
                    mm = nc.tensor.matmul(ps[:, 256 * rp:256 * rp + 256],
                                          QR[:, par, s, 2 * rp:2 * rp + 2, :].rearrange("p a k -> p (a k)"),
                                          KM[:, par, s, :, :].rearrange("p a k -> p (a k)"),
                                          start=False, stop=True, skip_group_check=True)
                mm.then_inc(p_s, 1)

            def turn(i, k):
                U = 8 * i + k
                ge(pe, g_norm, U + 1)
                ge(pe, a_pt, U - 1)
                for b in range(4):
                    mm = nc.tensor.transpose(T_ps[k % 2][:, 128 * b:128 * b + 128],
                                             PP[:, k % 4, 128 * b:128 * b + 128], ident[:, :])
                mm.then_inc(p_t, 1)

            def attend(i, k):
                U, P, T, s, par = 8 * i + k, 2 * i + k // 4, 4 * i + k // 2, k % 4, k // 4 % 2
                if s == 0:
                    ge(pe, a_v, P + 1)
                if s % 2 == 0:
                    ge(pe, a_at, T - 1)
                ge(pe, a_pt, U + 1)
                for b in range(4):
                    mm = nc.tensor.matmul(A_ps[k // 2 % 2][32 * b:32 * b + 32, 128 * (k % 2):128 * (k % 2) + 128],
                                          VM[:, par, s, 2 * b:2 * b + 2, :, :].rearrange("p a b c -> p (a b c)"),
                                          PT[:, k % 2, 128 * b:128 * b + 128], start=True, stop=True)
                mm.then_inc(p_pv, 1)

            def project(T, t, z_before):
                ge(pe, a_at, T + 1)
                ge(pe, v_x2, T)
                ge(pe, a_zt, z_before)
                for b in range(2):
                    for r2 in range(2):
                        mm = nc.tensor.matmul(J1[64 * b:64 * b + 64, 0:D], AT[:, t, b, 64 * r2:64 * r2 + 64],
                                              WOZ[:, r2, :], start=(r2 == 0), stop=(r2 == 1))
                mm.then_inc(p_w, 1)

            def turn_z(P, x2_before):
                ge(pe, a_z, P + 1)
                ge(pe, v_x2, x2_before)
                if isinstance(P, int):
                    ge(pe, a_zt, P)
                for k in range(2):
                    mm = nc.tensor.transpose(J1[:, 128 * k:128 * k + 128], ZZ[:, k, :], ident[:, :])
                mm.then_inc(p_zt, 1)

            def steps(i):
                static = isinstance(i, int)
                for u in range(8):
                    P, U, s, h = 2 * i + u // 4, 8 * i + u, u % 4, u // 4
                    more = not static or P + 1 < NP
                    if not static or U < NB:
                        scores(i, u)
                    if not static or 0 <= U - 3 < NB:
                        turn(i, u - 3)
                    if not static or 0 <= U - 4 < NB:
                        attend(i, u - 4)
                    if s == 0 and more:
                        pe.wait_ge(d_ct[(h + 1) % 2], 16 * i + 16 * (h + 1))
                        prep_xk(P + 1, (h + 1) % 2)
                    if s == 1 and more:
                        prep_q(P + 1)
                    if s == 2 and more:
                        prep_v(P + 1, (h + 1) % 2)
                    if s == 0 and (not static or 0 <= P - 2 < NP):
                        project(4 * i + (2 * h - 3), 1, P - 3)
                    if s == 2 and (not static or 0 <= P - 1 < NP):
                        project(4 * i + (2 * h - 2), 0, P - 3)
                    if s == 3 and (not static or 0 <= P - 3 < NP):
                        turn_z(P - 3, 4 * i + 2 * h - 1 if not static else min(2 * P - 1, NT))

            pe.wait_ge(g_const, 1)
            pe.wait_ge(v_setup, 1)
            pe.wait_ge(d_w, 64)
            pe.wait_ge(d_ct[0], 16)
            prep_xk(0, 0)
            prep_q(0)
            prep_v(0, 0)
            steps(0)
            steps(1)
            with pe.Fori(2, NB // 8 - 1) as i:
                steps(i)
            steps(NB // 8 - 1)
            steps(NB // 8)
            turn_z(NP - 1, NT)

            pe.wait_ge(d_late, 96)
            pe.wait_ge(v_zs, NP)
            pe.wait_ge(a_v, NP)
            nc.tensor.matmul(J0[:, 0:E], ZS[:, :], WR[:, :], start=True, stop=True).then_inc(p_r, 1)
            pe.wait_ge(v_r, 2)
            pe.wait_ge(a_zt, NP)
            nc.tensor.transpose(J1[0:E, 0:128], RL[:, CWR, :], ident[:, :])
            nc.tensor.matmul(A_ps[0][:, 0:E], before[:, :], RL[:, SEL, :], start=True, stop=True)
            nc.tensor.matmul(A_ps[1][0:E, 0:1], RL[:, SEL, :], ones[:, 0:1], start=True, stop=True).then_inc(p_r, 1)
            pe.wait_ge(v_r, 3)
            nc.tensor.matmul(J0[:, 0:E + 1], NEB[:, :], before[0:E, 0:E + 1], start=True, stop=True).then_inc(p_r, 1)
            pe.wait_ge(v_r, 4)
            nc.tensor.matmul(J0[0:1, 0:SLOTS], bcol[:, 0:1], OH[:, 0, :], start=True, stop=False)
            nc.tensor.matmul(J0[0:1, 0:SLOTS], bcol[:, 1:2], OHF, start=False, stop=True)
            nc.tensor.matmul(J1[:, 0:SLOTS], ones[:, :], OH[:, 1, :], start=True, stop=True).then_inc(p_r, 1)

            pe.nop().then_inc(p_h, 8)
            pe.nop().then_inc(p_o, 2)
            pe.wait_ge(v_r, 5)
            pe.wait_ge(g_w0, 2)
            with pe.Fori(0, E // 2) as e2:
                bounds = expert_bounds(mybir.EngineType.PE, e2)
                for par in range(2):
                    pe.wait_ge(v_w, 2 * e2 + (par + 1))
                    pe.nop().then_inc(p_begun, 1)
                    with pe.Fori(bounds[par], bounds[par + 1]) as g:
                        for half in range(2):
                            pe.wait_ge(g_lo, 2 * g + (half + 3))
                            for c in range(FC):
                                last = 8 * g + 4 * half + c + (3 if (half, c) in ((0, 0), (0, 1), (1, 2), (1, 3)) else 1)
                                pe.wait_ge(a_g, last)
                                cols, ps = slice(128 * c, 128 * c + 128), hidden_bank(half, c)[:, 0:HALF]
                                nc.tensor.matmul(ps, W1H[:, par, cols], XGH[:, half, :], start=True, stop=False)
                                nc.tensor.matmul(ps, W1H[:, par, cols], XGL[:, half, :], start=False, stop=False)
                                nc.tensor.matmul(ps, W1L[:, par, cols], XGH[:, half, :],
                                                 start=False, stop=True).then_inc(p_h, 1)
                        for half in range(2):
                            pe.wait_ge(v_c, 8 * g + (4 * half + 4))
                            ps = bank[6 + half][:, 0:HALF]
                            for c in range(FC):
                                pe.wait_ge(v_gl if c % 2 == 0 else g_gl, 4 * g + (2 * half + c // 2 + 5))
                                cols = slice(128 * c, 128 * c + 128)
                                nc.tensor.matmul(ps, W2H[:, par, cols], GH[:, half, c, :], start=(c == 0), stop=False)
                                nc.tensor.matmul(ps, W2H[:, par, cols], GL[:, half, c, :], start=False, stop=False)
                                mm = nc.tensor.matmul(ps, W2L[:, par, cols], GH[:, half, c, :],
                                                      start=False, stop=(c == FC - 1))
                            mm.then_inc(p_o, 1)

            blocks = pe.value_load(STI[0:1, E:E + 1], min_val=1, max_val=MAXBLK)
            pe.wait_ge(v_c, 8 * blocks + 8)
            for t in range(NT):
                ge(pe, a_yn, t - 7)
                ps, k = bank[t % 8][:, 0:D], t // 4 % 4
                ge(pe, a_cw, t // 4 + 1)
                nc.tensor.matmul(ps, CWX[:, k, 128 * (t % 4):128 * (t % 4) + 128], B2A[:, :], start=True, stop=False)
                nc.tensor.matmul(ps, YT[:, 128 * t:128 * t + 128], ident[:, :],
                                 start=False, stop=True).then_inc(p_y, 1)

        @block.scalar
        def _(act):
            def prep_v(P, par):
                act.wait_ge(p_v, P + 1)
                ge(act, p_pv, 4 * P - 4)
                for j2 in range(2):
                    rows = slice(64 * j2, 64 * j2 + 64)
                    ins = nc.scalar.activation(VM[rows, par, :, :, j2, :].rearrange("p b g d -> p (b g) d"),
                                               J0[rows, 0:256].rearrange("p (n d) -> p n d", d=HD), ACT.Copy)
                    ins.then_inc(a_vh if j2 == 0 else a_v, 1)

            def prep_xk(P):
                act.wait_ge(p_xk, P + 1)
                ge(act, g_km, P)
                ge(act, p_q, P)
                nc.scalar.activation(XK[:, :], J0[:, :], ACT.Copy).then_inc(a_xk, 1)

            def prep_q(P, par):
                act.wait_ge(p_q, P + 1)
                ge(act, p_s, 4 * P - 4)
                for r in range(4):
                    rows = slice(32 * r, 32 * r + 32)
                    nc.scalar.activation(QR[rows, par, :, r, :], J0[rows, 0:256].rearrange("p (b q) -> p b q", q=S),
                                         ACT.Copy).then_inc(a_q if r == 3 else a_qp, 1)

            def norm1(P):
                act.wait_ge(v_sh1, P + 1)
                ge(act, p_xk, P)
                for k in range(2):
                    nc.scalar.activation(XN[:, k, :], X[:, bass.ds(2 * P + k, 1), :].rearrange("p o d -> p (o d)"),
                                         ACT.Identity, bias=SH1[:, k:k + 1],
                                         scale=RS1[:, k:k + 1]).then_inc(a_xnp if k == 0 else a_xn, 1)

            def norm2(P):
                act.wait_ge(v_sh2, P + 1)
                ge(act, p_zt, P)
                for k in range(2):
                    nc.scalar.activation(ZZ[:, k, :], X[:, bass.ds(2 * P + k, 1), :].rearrange("p o d -> p (o d)"),
                                         ACT.Identity, bias=SH2[:, k:k + 1],
                                         scale=RS2[:, k:k + 1]).then_inc(a_zp if k == 0 else a_z, 1)

            def keep_z(P):
                act.wait_ge(p_zt, P + 1)
                nc.scalar.activation(ZT[:, bass.ds(P * 256, 256)], J1[:, 0:256], ACT.Copy).then_inc(a_zt, 1)

            def steps(i):
                static = isinstance(i, int)
                for u in range(8):
                    P, U, s, h = 2 * i + u // 4, 8 * i + u, u % 4, u // 4
                    more = not static or P + 1 < NP
                    if s == 0 and (not static or 0 <= P - 4 < NP):
                        keep_z(P - 4)
                    if s == 0 and more:
                        norm1(P + 1)
                    if not static or 0 <= U - 1 < NB:
                        act.wait_ge(v_sub, U)
                        ge(act, p_t, U - 4)
                        nc.scalar.activation(PP[:, (u - 1) % 4, :], SS[:, (u - 1) % 2, :], ACT.Exp,
                                             scale=SCALE).then_inc(a_exp, 1)
                    if s == 1 and more:
                        prep_xk(P + 1)
                    if s == 2 and more:
                        prep_q(P + 1, (h + 1) % 2)
                    if not static or 0 <= U - 3 < NB:
                        act.wait_ge(p_t, U - 2)
                        ge(act, p_pv, U - 4)
                        nc.scalar.activation(PT[:, (u - 3) % 2, :], T_ps[(u - 3) % 2][:, :],
                                             ACT.Copy).then_inc(a_pt, 1)
                    if s == 3 and more:
                        prep_v(P + 1, (h + 1) % 2)
                    if s == 1 and (not static or 0 <= P - 3 < NP):
                        norm2(P - 3)
                    if u % 2 == 1 and (not static or 0 <= U - 5 < NB):
                        t = (u - 5) // 2 % 2
                        act.wait_ge(p_pv, U - 3)
                        ge(act, p_w, 4 * i + (u // 2 - 3))
                        nc.scalar.activation(AT[:, t, :, :].rearrange("p b q -> p (b q)"),
                                             A_ps[t][:, 0:256], ACT.Copy).then_inc(a_at, 1)

            act.wait_ge(v_setup, 3)
            norm1(0)
            prep_xk(0)
            prep_q(0, 0)
            prep_v(0, 0)
            steps(0)
            steps(1)
            with act.Fori(2, NB // 8 - 1) as i:
                steps(i)
            steps(NB // 8 - 1)
            steps(NB // 8)
            keep_z(NP - 2)
            norm2(NP - 1)
            keep_z(NP - 1)

            def split_hi(loads, par):
                act.wait_ge(d_ex[par], 32 * loads)
                nc.scalar.activation(W1H[:, par, :], W1R[:, par, :], ACT.Copy).then_inc(a_whi, 1)
                nc.scalar.activation(W2H[:, par, :], W2R[:, par, :], ACT.Copy).then_inc(a_whi, 1)

            split_hi(1, 0)
            act.wait_ge(g_const, 3)
            act.wait_ge(a_zt, NP)
            nc.scalar.activation(YT[:, :], ZT[:, :], ACT.Copy).then_inc(a_yt, 1)
            act.wait_ge(v_r, 1)
            nc.scalar.activation(RL[:, EXPW, :], RL[:, LOGIT, :], ACT.Exp, bias=RV[:, 1:2]).then_inc(a_r, 1)
            act.wait_ge(v_rt, 1)
            nc.scalar.activation(RV[:, 9:10], RV[:, 8:9], ACT.Exp).then_inc(a_r, 1)

            act.nop().then_inc(a_g, 8)
            act.wait_ge(v_r, 5)
            def gather_hi(g, half):
                act.wait_ge(d_xr[half], 64 * g + 64)
                act.wait_ge(p_h, 8 * g + (4 * half + 4))
                nc.scalar.activation(XGH[:, half, :], XR[:, half, :], ACT.Copy).then_inc(a_hi, 1)

            nc.scalar.activation(RV[:, 15:16], RV[:, 9:10], ACT.Gelu)
            for half in range(2):
                gather_hi(0, half)
            with act.Fori(0, E // 2) as e2:
                bounds = expert_bounds(mybir.EngineType.Activation, e2)
                for par in range(2):
                    settle(act, v_setup)
                    act.wait_ge(p_o, 2 * bounds[par] + 2)
                    split_hi(e2 + (par + 1), 1 - par)
                    act.wait_ge(v_b1, 2 * e2 + (par + 1))
                    with act.Fori(bounds[par], bounds[par + 1]) as g:
                        for half in range(2):
                            for c in range(FC):
                                ps, b1e = hidden_bank(half, c)[:, 0:HALF], B1E[:, par, c:c + 1]
                                act.wait_ge(p_h, 8 * g + (4 * half + c + 9))
                                if c == 0:
                                    act.wait_ge(p_o, 2 * g + (half + 1))
                                act.wait_ge(v_gl if c % 2 == 0 else g_gl, 4 * g + (2 * half + c // 2 + 1))
                                if c % 2 == 1:
                                    nc.scalar.activation(GH[:, half, c, :], ps, ACT.Gelu, bias=b1e).then_inc(a_gh, 1)
                                nc.scalar.activation(G[:, half, c, :], ps, ACT.Gelu, bias=b1e).then_inc(a_g, 1)
                            gather_hi(g + 1, half)

            def token_weights(n, k):
                nc.scalar.activation(CWX[:, k, :].rearrange("p (b q) -> p b q", q=S),
                                     CWT[:, bass.ds(8 * n, 8)].unsqueeze(2).to_broadcast([E, 8, S]),
                                     ACT.Copy).then_inc(a_cw, 1)

            blocks = load_values(mybir.EngineType.Activation, STI[0:1, E:E + 1], 1, MAXBLK)[0]
            act.wait_ge(v_c, 8 * blocks + 8)
            act.wait_ge(g_lo, 2 * blocks + 4)
            token_weights(0, 0)
            with act.Fori(0, 4) as o:
                for k in range(4):
                    token_weights(4 * o + (k + 1), (k + 1) % 4)
                    act.wait_ge(g_nb3, 4 * o + (k + 1))
                    act.wait_ge(d_out[k], 16 * o + 16)
                    for m in range(4):
                        nc.scalar.activation(YN[:, k, m, :], bank[(4 * k + m) % 8][:, 0:D], ACT.Identity,
                                             bias=NB3[:, k, m:m + 1], scale=RS3[:, k, m:m + 1]).then_inc(a_yn, 1)

        @block.vector
        def _(dve):
            chain = [0]

            def link(ins):
                chain[0] += 1
                ins.then_inc(v_chain, 1)
                dve.wait_ge(v_chain, chain[0])

            def stats1(P):
                n = 2 * P + 2
                if not isinstance(P, int):
                    dve.wait_ge(v_max, n)
                settle(dve, v_setup)
                ge(dve, v_sh1, P)
                for k in range(2):
                    nc.vector.bn_stats(ST1[:, k, :], X[:, bass.ds(2 * P + k, 1), :].rearrange("p o d -> p (o d)")
                                       ).then_inc(v_bn1, 1)
                settle(dve, v_setup)
                dve.wait_ge(v_bn1, n)
                for k in range(2):
                    nc.vector.bn_aggr(MV1[:, k, :], ST1[:, k, :]).then_inc(v_mv1, 1)

            def shift1(P):
                dve.wait_ge(g_rs1, P + 1)
                nc.vector.scalar_tensor_tensor(SH1[:, :], MV1[:, :, 0], -1.0, RS1[:, :],
                                               ALU.mult, ALU.mult).then_inc(v_sh1, 1)

            def shift2(P, h):
                dve.wait_ge(g_rs2, P + 1)
                nc.vector.scalar_tensor_tensor(SH2[:, :], MV2[:, 2 * h:2 * h + 2, 0], -1.0, RS2[:, :],
                                               ALU.mult, ALU.mult).then_inc(v_sh2, 1)

            def residual(T):
                xt = X[:, bass.ds(T, 1), :].rearrange("p o d -> p (o d)")
                dve.wait_ge(p_w, T + 1)
                nc.vector.tensor_tensor(xt, J1[:, 0:D], xt, ALU.add).then_inc(v_x2, 1)

            def stats2(T, k):
                xt = X[:, bass.ds(T, 1), :].rearrange("p o d -> p (o d)")
                settle(dve, v_setup)
                dve.wait_ge(v_x2, T + 1)
                nc.vector.bn_stats(ST2[:, k, :], xt).then_inc(v_bn2, 1)

            def mean2(T, slot, k):
                settle(dve, v_setup)
                dve.wait_ge(v_bn2, T + 1)
                nc.vector.bn_aggr(MV2[:, slot, :], ST2[:, k, :]).then_inc(v_mv2, 1)

            def zsum(P):
                dve.wait_ge(a_zt, P + 1)
                nc.vector.reduce_sum(ZS[:, bass.ds(4 * P, 4)],
                                     ZT[:, bass.ds(256 * P, 256)].rearrange("p (b q) -> p b q", q=S),
                                     AX.X).then_inc(v_zs, 1)

            def steps(i):
                static = isinstance(i, int)
                for u in range(8):
                    P, U, s, h = 2 * i + u // 4, 8 * i + u, u % 4, u // 4
                    if s == 1:
                        T, slot, k2, late = 4 * i + (2 * h - 3), (2 * h + 1) % 4, 1, not static or 0 <= P - 2 < NP
                    else:
                        T, slot, k2, late = 4 * i + (2 * h - 2), (2 * h - 2) % 4, 0, not static or 0 <= P - 1 < NP
                    late = late and s % 2 == 1
                    before, now, k = not static or 0 <= U - 1 < NB, not static or U < NB, (u - 1) % 8
                    if late:
                        residual(T)
                    if now:
                        ps = S_ps[u % 2][:, :].rearrange("p (n k) -> p n k", k=S)
                        dve.wait_ge(p_s, U + 1)
                        nc.vector.reduce_max(MX[:, u % 2, :], ps, AX.X).then_inc(v_max, 1)
                    if before:
                        dve.wait_ge(a_exp, U)
                        nc.vector.reduce_sum(SM[:, k % 2, :], PP[:, k % 4, :].rearrange("p (n k) -> p n k", k=S),
                                             AX.X).then_inc(v_sum, 1)
                    if late:
                        stats2(T, k2)
                    if now:
                        dve.wait_ge(v_max, U + 1)
                        ge(dve, a_exp, U - 1)
                        nc.vector.tensor_tensor(SS[:, u % 2, :].rearrange("p (n k) -> p n k", k=S), ps,
                                                MX[:, u % 2, :].unsqueeze(2).to_broadcast([128, 8, S]),
                                                ALU.subtract).then_inc(v_sub, 1)
                    if before:
                        dve.wait_ge(v_sum, U)
                        ge(dve, g_norm, U - 2)
                        nc.vector.reciprocal(RC[:, k % 2, :], SM[:, k % 2, :]).then_inc(v_rcp, 1)
                    if late:
                        mean2(T, slot, k2)
                    if s == 0 and (not static or P + 2 < NP):
                        dve.wait_ge(d_x, 16 * i + 32)
                        stats1(P + 2)
                    if s == 2 and (not static or P + 2 < NP):
                        shift1(P + 2)
                    if s == 2 and (not static or 0 <= P - 4 < NP):
                        zsum(P - 4)
                    if s == 3 and (not static or 0 <= P - 2 < NP):
                        shift2(P - 2, h)

            dve.wait_ge(g_const, 1)
            link(nc.vector.tensor_reduce(jmask[:, :], grp8[:, :].rearrange("p (r j) -> p j r", j=4), AX.X, ALU.add))
            link(nc.vector.tensor_reduce(r2mask[:, :], grp16[:, :].rearrange("p (a b) -> p b a", b=2), AX.X, ALU.add))
            dve.wait_ge(d_w, 64)
            link(nc.vector.tensor_scalar(WOZ[:, 0, :], WO[:, :], r2mask[:, 0:1], None, ALU.mult))
            nc.vector.tensor_scalar(WOZ[:, 1, :], WO[:, :], r2mask[:, 1:2], None, ALU.mult).then_inc(v_setup, 1)
            nc.vector.memset(VM[:, :, :, :, :, :], 0.0).then_inc(v_setup, 1)
            nc.vector.memset(QR[:, :, :, :, :], 0.0).then_inc(v_setup, 1)
            dve.wait_ge(d_x, 16)
            stats1(0)
            shift1(0)
            stats1(1)
            shift1(1)
            steps(0)
            steps(1)
            with dve.Fori(2, NB // 8 - 1) as i:
                steps(i)
            steps(NB // 8 - 1)
            steps(NB // 8)
            zsum(NP - 2)
            zsum(NP - 1)

            def pick(w, onehot, top, least):
                link(nc.vector.reduce_max(RV[:, top:top + 1], RL[:, w, :], AX.X))
                link(nc.vector.tensor_scalar(RL[:, TIE, :], RL[:, w, :], RV[:, top:top + 1], None, ALU.is_equal))
                link(nc.vector.scalar_tensor_tensor(RL[:, CAND, :], RL[:, TIE, :], -float(E), iota_e[:, :],
                                                    ALU.mult, ALU.add))
                link(nc.vector.tensor_reduce(RV[:, least:least + 1], RL[:, CAND, :], AX.X, ALU.min))
                link(nc.vector.tensor_scalar(RL[:, onehot, :], RL[:, CAND, :], RV[:, least:least + 1], None,
                                             ALU.is_equal))

            dve.wait_ge(g_const, 2)
            dve.wait_ge(p_r, 1)
            link(nc.vector.scalar_tensor_tensor(RL[:, LOGIT, :], J0[:, 0:E], 1.0 / S, BR[:, :], ALU.mult, ALU.add))
            link(nc.vector.reduce_max(RV[:, 0:1], RL[:, LOGIT, :], AX.X))
            nc.vector.tensor_scalar(RV[:, 1:2], RV[:, 0:1], -1.0, None, ALU.mult).then_inc(v_r, 1)
            dve.wait_ge(a_r, 1)
            link(nc.vector.reduce_sum(RV[:, 2:3], RL[:, EXPW, :], AX.X))
            link(nc.vector.reciprocal(RV[:, 3:4], RV[:, 2:3]))
            link(nc.vector.tensor_scalar(RL[:, PROB, :], RL[:, EXPW, :], RV[:, 3:4], None, ALU.mult))
            pick(PROB, PICK1, 4, 5)
            link(nc.vector.scalar_tensor_tensor(RL[:, REST, :], RL[:, PICK1, :], -4.0, RL[:, PROB, :],
                                                ALU.mult, ALU.add))
            pick(REST, PICK2, 6, 7)
            nc.vector.tensor_tensor(RV[:, 8:9], RV[:, 6:7], RV[:, 4:5], ALU.subtract).then_inc(v_rt, 1)
            dve.wait_ge(a_r, 2)
            link(nc.vector.tensor_scalar(RV[:, 10:11], RV[:, 9:10], 1.0, None, ALU.add))
            link(nc.vector.reciprocal(RV[:, 11:12], RV[:, 10:11]))
            link(nc.vector.tensor_tensor(RV[:, 12:13], RV[:, 9:10], RV[:, 11:12], ALU.mult))
            link(nc.vector.tensor_scalar(RL[:, TIE, :], RL[:, PICK1, :], RV[:, 11:12], None, ALU.mult))
            link(nc.vector.scalar_tensor_tensor(RL[:, CWR, :], RL[:, PICK2, :], RV[:, 12:13], RL[:, TIE, :],
                                                ALU.mult, ALU.add))
            nc.vector.tensor_tensor(RL[:, SEL, :], RL[:, PICK1, :], RL[:, PICK2, :], ALU.add).then_inc(v_r, 1)
            dve.wait_ge(p_r, 2)
            link(nc.vector.tensor_scalar(NEI[:, 0:1], A_ps[1][0:E, 0:1], float(GB - 1), None, ALU.add))
            link(nc.vector.tensor_scalar(NEI[:, 1:2], NEI[:, 0:1], 3, None, ALU.arith_shift_right))
            link(nc.vector.tensor_scalar(NE1[:, 0:1], NEI[:, 1:2], 1.0, None, ALU.max))
            link(nc.vector.tensor_copy(RL[:, POS, :], A_ps[0][:, 0:E]))
            link(nc.vector.tensor_copy(CWT[:, 0:128], J1[0:E, 0:128]))
            nc.vector.tensor_scalar(NEB[:, :], ones[0:E, :], NE1[:, 0:1], None, ALU.mult).then_inc(v_r, 1)
            dve.wait_ge(p_r, 3)
            link(nc.vector.tensor_copy(STI[:, :], J0[:, 0:E + 1]))
            link(nc.vector.scalar_tensor_tensor(RL[:, SLOT, :], J0[:, 0:E], float(GB), RL[:, POS, :],
                                                ALU.mult, ALU.add))
            for n, onehot in enumerate((PICK1, PICK2)):
                link(nc.vector.tensor_tensor(RL[:, TIE, :], RL[:, SLOT, :], RL[:, onehot, :], ALU.mult))
                link(nc.vector.reduce_sum(RV[:, 13 + n:14 + n], RL[:, TIE, :], AX.X))
                link(nc.vector.tensor_scalar(OH[:, n, :], iota_s[:, :], RV[:, 13 + n:14 + n], None, ALU.is_equal))
            link(nc.vector.tensor_scalar(CW[:, :], OH[:, 0, :], RV[:, 11:12], None, ALU.mult))
            link(nc.vector.tensor_tensor(OH[:, 0, :], OH[:, 0, :], OH[:, 1, :], ALU.add))
            link(nc.vector.tensor_tensor(OHF, OH[:, 0, :], iota_f[:, :], ALU.mult))
            nc.vector.scalar_tensor_tensor(OH[:, 1, :], OH[:, 1, :], RV[:, 12:13], CW[:, :],
                                           ALU.mult, ALU.add).then_inc(v_r, 1)
            dve.wait_ge(v_r, 4)
            dve.wait_ge(p_r, 4)
            link(nc.vector.scalar_tensor_tensor(IDX[:, :], J0[0:1, 0:SLOTS], float(NOBATCH), iota_f[0:1, :],
                                                ALU.add, ALU.add))
            nc.vector.tensor_copy(CW[:, :], J1[:, 0:SLOTS]).then_inc(v_r, 1)

            dve.nop().then_inc(v_gl, 4)
            dve.nop().then_inc(v_c, 8)
            dve.nop().then_inc(v_w, 1)
            nc.vector.tensor_copy(B1E[:, 0, :], B1A[:, 0, :]).then_inc(v_b1, 1)
            dve.wait_ge(a_yt, 1)
            with dve.Fori(0, E // 2) as e2:
                bounds = expert_bounds(mybir.EngineType.DVE, e2)
                for par in range(2):
                    other = 1 - par
                    dve.wait_ge(a_whi, 4 * e2 + (2 * par + 4))
                    nc.vector.tensor_copy(B1E[:, other, :],
                                          B1A[:, bass.ds(2 * e2 + (par + 1), 1), :].rearrange("p o c -> p (o c)")
                                          ).then_inc(v_b1, 1)
                    nc.vector.tensor_tensor(W1L[:, other, :], W1R[:, other, :], W1H[:, other, :],
                                            ALU.subtract).then_inc(v_wl, 1)
                    nc.vector.tensor_tensor(W2L[:, other, :], W2R[:, other, :], W2H[:, other, :],
                                            ALU.subtract).then_inc(v_w, 1)
                    with dve.Fori(bounds[par], bounds[par + 1]) as g:
                        for half in range(2):
                            dve.wait_ge(p_o, 2 * g + (half + 1))
                            for c in range(0, FC, 2):
                                dve.wait_ge(a_g, 8 * g + (4 * half + c + 9))
                                nc.vector.tensor_copy(GH[:, half, c, :], G[:, half, c, :]).then_inc(v_gh, 1)
                                dve.wait_ge(v_gh, 4 * g + (2 * half + c // 2 + 1))
                                nc.vector.tensor_tensor(GL[:, half, c, :], G[:, half, c, :], GH[:, half, c, :],
                                                        ALU.subtract).then_inc(v_gl, 1)
                        for half in range(2):
                            b = half_batches(mybir.EngineType.DVE, g, half)
                            dve.wait_ge(p_o, 2 * g + (half + 3))
                            dve.wait_ge(v_c, 8 * g + (4 * half + 8))
                            for k in range(4):
                                yt = YT[:, bass.ds(b[k] * S, S)]
                                nc.vector.scalar_tensor_tensor(
                                    yt, bank[6 + half][:, S * k:S * k + S], CW[:, bass.ds(8 * g + (4 * half + k), 1)],
                                    yt, ALU.mult, ALU.add).then_inc(v_c, 1)

            def stats3(o, k):
                for m in range(4):
                    settle(dve, v_setup)
                    dve.wait_ge(p_y, 16 * o + (4 * k + m + 1))
                    nc.vector.bn_stats(ST3[:, k, m, :], bank[(4 * k + m) % 8][:, 0:D]).then_inc(v_bn3, 1)
                for m in range(4):
                    settle(dve, v_setup)
                    dve.wait_ge(v_bn3, 16 * o + (4 * k + m + 1))
                    nc.vector.bn_aggr(MV3[:, k, m, :], ST3[:, k, m, :]).then_inc(v_mv3, 1)

            def finish(o, k, T):
                dve.wait_ge(g_gam, 4 * o + (k + 1))
                nc.vector.tensor_tensor(YN[:, k, :, :], YN[:, k, :, :], X[:, bass.ds(T, 4), :],
                                        ALU.add).then_inc(v_out, 1)

            dve.wait_ge(g_xb, NP)
            stats3(0, 0)
            for k in range(1, 4):
                stats3(0, k)
                finish(0, k - 1, 4 * k - 4)
            with dve.Fori(1, 4) as o:
                for k in range(4):
                    stats3(o, k)
                    if k == 0:
                        dve.wait_ge(g_gam, 4 * o)
                        nc.vector.tensor_tensor(YN[:, 3, :, :], YN[:, 3, :, :], X[:, bass.ds(16 * o - 4, 4), :],
                                                ALU.add).then_inc(v_out, 1)
                    else:
                        finish(o, k - 1, 16 * o + (4 * k - 4))
            finish(3, 3, 60)

        @block.gpsimd
        def _(pool):
            chain = [0]

            def link(ins):
                chain[0] += 1
                ins.then_inc(g_chain, 1)
                pool.wait_ge(g_chain, chain[0])

            def keep(t, op, base, pattern, mult, fill=0.0):
                link(nc.gpsimd.affine_select(out=t, in_=t, compare_op=op, fill=fill, base=base, pattern=pattern,
                                             channel_multiplier=mult))

            for t, v in ((ident[:, :], 0.0), (cmask[:, :, :], 0.0), (grp8[:, :], 1.0), (grp16[:, :], 1.0),
                         (minus_half[:, :], -0.5), (minus_one[:, :], -1.0), (eps[:, :], EPS)):
                link(nc.gpsimd.memset(t, v))
            keep(ident[:, :], ALU.not_equal, 0, [[-1, 128]], 1, 1.0)
            link(nc.gpsimd.tensor_copy(identb[:, :], ident[:, :]))
            for q0 in (0, 64):
                keep(cmask[q0:q0 + 64, :, :], ALU.is_ge, 0, [[0, 8], [-1, S]], 1, MASKED)
            keep(grp8[:, :], ALU.is_ge, 0, [[-8, 16]], 1)
            keep(grp8[:, :], ALU.is_ge, 7, [[8, 16]], -1)
            keep(grp16[:, :], ALU.is_ge, 0, [[-16, 8]], 1)
            keep(grp16[:, :], ALU.is_ge, 15, [[16, 8]], -1)
            pool.nop().then_inc(g_const, 1)

            def rstd(mv, rs, eps_sem, rs_sem, n):
                nc.gpsimd.tensor_tensor(rs, mv, eps[:, 0:rs.shape[-1]], ALU.add).then_inc(eps_sem, 1)
                pool.wait_ge(eps_sem, n)
                nc.gpsimd.tensor_tensor(rs, rs, minus_half[:, 0:rs.shape[-1]], ALU.pow).then_inc(rs_sem, 1)

            def rstd1(P):
                pool.wait_ge(v_mv1, 2 * P + 2)
                ge(pool, a_xn, P)
                rstd(MV1[:, :, 1], RS1[:, :], g_eps1, g_rs1, P + 1)

            def rstd2(P, h):
                pool.wait_ge(v_mv2, 2 * P + 2)
                ge(pool, a_z, P)
                rstd(MV2[:, 2 * h:2 * h + 2, 1], RS2[:, :], g_eps2, g_rs2, P + 1)

            def spread_k(P, par, batches):
                pool.wait_ge(a_xk, P + 1)
                ge(pool, p_s, 4 * P - 4)
                for b in batches:
                    ins = nc.gpsimd.tensor_tensor(KM[:, par, b, :, :],
                                                  XK[:, 256 + S * b:256 + S * b + S].unsqueeze(1)
                                                  .to_broadcast([128, 4, S]),
                                                  jmask[:, :].unsqueeze(2).to_broadcast([128, 4, S]), ALU.mult)
                    ins.then_inc(g_km if b == 3 else g_kmb, 1)

            def x_plus_beta(P, tile):
                pool.wait_ge(a_z, P + 1)
                xp = X[:, bass.ds(tile, 2), :]
                nc.gpsimd.tensor_tensor(xp, xp, BET[:, :].unsqueeze(1).to_broadcast([128, 2, D]),
                                        ALU.add).then_inc(g_xb, 1)

            def steps(i):
                static = isinstance(i, int)
                for u in range(8):
                    P, U, s, h = 2 * i + u // 4, 8 * i + u, u % 4, u // 4
                    more = not static or P + 1 < NP
                    if s in (1, 2) and more:
                        spread_k(P + 1, (h + 1) % 2, (2 * s - 2, 2 * s - 1))
                    if not static or 0 <= U - 1 < NB:
                        k = (u - 1) % 8
                        pp = PP[:, k % 4, :].rearrange("p (n k) -> p n k", k=S)
                        pool.wait_ge(v_rcp, U)
                        nc.gpsimd.tensor_tensor(pp, pp, RC[:, k % 2, :].unsqueeze(2).to_broadcast([128, 8, S]),
                                                ALU.mult).then_inc(g_norm, 1)
                    if s == 0 and (not static or 0 <= P - 4 < NP):
                        x_plus_beta(P - 4, 4 * i + (2 * h - 8))
                    if s == 1 and (not static or P + 2 < NP):
                        rstd1(P + 2)
                    if s == 2 and (not static or 0 <= P - 2 < NP):
                        rstd2(P - 2, h)

            pool.wait_ge(v_chain, 2)
            rstd1(0)
            rstd1(1)
            spread_k(0, 0, range(4))
            link(nc.gpsimd.memset(ones[:, :], 1.0))
            link(nc.gpsimd.memset(before[:, :], 1.0))
            keep(before[:, :], ALU.is_gt, 0, [[1, 128]], -1)
            link(nc.gpsimd.iota(IOT[:, :], pattern=[[1, SLOTS]], base=0, channel_multiplier=0))
            link(nc.gpsimd.tensor_copy(iota_s[:, :], IOT[:, :]))
            link(nc.gpsimd.tensor_copy(iota_e[:, :], IOT[:, 0:E]))
            link(nc.gpsimd.iota(IOT[:, 0:1], pattern=[[0, 1]], base=-NOBATCH, channel_multiplier=1))
            link(nc.gpsimd.tensor_copy(bcol[:, 0:1], IOT[:, 0:1]))
            link(nc.gpsimd.memset(bcol[:, 1:2], -1.0))
            link(nc.gpsimd.iota(IOT[:, :], pattern=[[0, SLOTS // GB], [1, GB]], base=0, channel_multiplier=0))
            link(nc.gpsimd.tensor_copy(iota_f[:, :], IOT[:, :]))
            pool.nop().then_inc(g_const, 1)
            pool.wait_ge(d_late, 96)
            steps(0)
            steps(1)
            with pool.Fori(2, NB // 8 - 1) as i:
                steps(i)
            steps(NB // 8 - 1)
            steps(NB // 8)
            x_plus_beta(NP - 2, NT - 4)
            x_plus_beta(NP - 1, NT - 2)
            for t in (ZT[:, NB * S:], B1A[:, E, :], CWT[:, 128:]):
                link(nc.gpsimd.memset(t, 0.0))
            pool.nop().then_inc(g_const, 1)

            pool.wait_ge(a_whi, 2)
            nc.gpsimd.tensor_tensor(W1L[:, 0, :], W1R[:, 0, :], W1H[:, 0, :], ALU.subtract).then_inc(g_w0, 1)
            nc.gpsimd.tensor_tensor(W2L[:, 0, :], W2R[:, 0, :], W2H[:, 0, :], ALU.subtract).then_inc(g_w0, 1)
            pool.nop().then_inc(g_lo, 2)
            pool.nop().then_inc(g_gl, 4)

            def gather_lo(g, half):
                pool.wait_ge(a_hi, 2 * g + (half + 1))
                nc.gpsimd.tensor_tensor(XGL[:, half, :], XR[:, half, :], XGH[:, half, :],
                                        ALU.subtract).then_inc(g_lo, 1)

            for half in range(2):
                gather_lo(0, half)
            pool.wait_ge(v_r, 5)
            blocks = pool.value_load(STI[0:1, E:E + 1], min_val=1, max_val=MAXBLK)
            with pool.Fori(0, blocks) as g:
                for half in range(2):
                    pool.wait_ge(p_o, 2 * g + (half + 1))
                    for c in range(1, FC, 2):
                        pool.wait_ge(a_g, 8 * g + (4 * half + c + 9))
                        nc.gpsimd.tensor_tensor(GL[:, half, c, :], G[:, half, c, :], GH[:, half, c, :],
                                                ALU.subtract).then_inc(g_gl, 1)
                    gather_lo(g + 1, half)

            with pool.Fori(0, 4) as o:
                for k in range(4):
                    pool.wait_ge(v_mv3, 16 * o + (4 * k + 4))
                    rstd(MV3[:, k, :, 1], RS3[:, k, :], g_eps3, g_rs3, 4 * o + (k + 1))
                    pool.wait_ge(g_rs3, 4 * o + (k + 1))
                    nc.gpsimd.tensor_tensor(NB3[:, k, :], MV3[:, k, :, 0], RS3[:, k, :], ALU.mult).then_inc(g_nb3a, 1)
                    pool.wait_ge(g_nb3a, 4 * o + (k + 1))
                    nc.gpsimd.tensor_tensor(NB3[:, k, :], NB3[:, k, :], minus_one[:, :], ALU.mult).then_inc(g_nb3, 1)
                    pool.wait_ge(a_yn, 16 * o + (4 * k + 4))
                    nc.gpsimd.tensor_tensor(YN[:, k, :, :], YN[:, k, :, :],
                                            GAM[:, :].unsqueeze(1).to_broadcast([128, 4, D]),
                                            ALU.mult).then_inc(g_gam, 1)


def kernel(**inputs):
    import concourse.bacc as bacc
    from concourse.bass_utils import run_bass_kernel_spmd

    a = {k: np.asarray(v) for k, v in inputs.items()}
    wvT = a["L0_xattn_Wv"].T.reshape(D, 4, 2, 2, HD)
    wv = wvT.transpose(0, 3, 1, 2, 4)
    wv = wv.reshape(D, 2, 2, 2, 2, HD).transpose(0, 1, 2, 4, 3, 5)
    woT = a["L0_xattn_Wo"].T.reshape(2, 2, 2, 2, HD, D)
    arrays = {
        "x": a["x"].reshape(NB * S, D),
        "ctxT": a["ctx_1024"].reshape(NB * S, D).T,
        "wq": a["L0_xattn_Wq"].T,
        "wk": a["L0_xattn_Wk"].T,
        "wv": wv.reshape(D, 2, D // 2),
        "wo": woT.transpose(0, 2, 1, 3, 4, 5).reshape(D, D),
        "w1": a["L0_ffn_W1"],
        "b1": a["L0_ffn_b1"].reshape(E, FC, 128).transpose(2, 0, 1),
        "w2": a["L0_ffn_W2"],
        "b2": a["L0_ffn_b2"],
        "wr": a["L0_ffn_Wr"],
        "br": a["L0_ffn_br"],
        "gamma": a["L0_ffn_gamma"],
        "beta": a["L0_ffn_beta"],
    }
    arrays = {k: np.ascontiguousarray(v) for k, v in arrays.items()}
    nc = bacc.Bacc("TRN2", target_bir_lowering=False, num_devices=1)
    args = {k: nc.dram_tensor("in_" + k, v.shape, F32, kind="ExternalInput").ap() for k, v in arrays.items()}
    out = nc.dram_tensor("out", (NB * S, D), F32, kind="ExternalOutput").ap()
    build(nc, **args, out=out)
    r = run_bass_kernel_spmd(nc, [{"in_" + k: v for k, v in arrays.items()}], core_ids=[0])
    return r.results[0]["out"].reshape(NB, S, D)
```

```python
from contextlib import ExitStack

import numpy as np

import concourse.bass as bass
from concourse import mybir

F32 = mybir.dt.float32
F32R = mybir.dt.float32r
BF16 = mybir.dt.bfloat16
I32 = mybir.dt.int32
ALU = mybir.AluOpType
ACT = mybir.ActivationFunctionType
AX = mybir.AxisListType

NB, S, D = 128, 64, 128
H, HD = 16, 8
E, F = 8, 512
FC = F // 128
SCALE = HD ** -0.5
EPS = 1e-5
MASKED = -1e30
NT = NB // 2
NP = NT // 2
GB = 8
HALF = GB // 2 * S
MAXBLK = (2 * NB + (GB - 1) * E) // GB
SLOTS = (MAXBLK + 1) * GB
NOBATCH = NB


def ge(eng, sem, n):
    if isinstance(n, int) and n <= 0:
        return
    eng.wait_ge(sem, n)


LOGIT, EXPW, PROB, TIE, CAND, PICK1, REST, PICK2, CWR, SEL, POS, SLOT = range(12)


def settle(eng, sem):
    eng.wait_ge(sem, 1)


def build(nc, x, ctxT, wq, wk, wv, wo, w1, b1, w2, b2, wr, br, gamma, beta, out):
    es = ExitStack()
    with es:
        def sb(name, shape, dt=F32):
            return es.enter_context(nc.sbuf_tensor(name, shape, dt))

        def sem(name):
            return es.enter_context(nc.semaphore(name))

        X = sb("x_res", [128, NT, D])
        ZT = sb("zT", [128, (NB + GB) * S])
        YT = sb("yT", [128, (NB + GB) * S])
        W1R = sb("w1_raw", [128, 2, F])
        W2R = sb("w2_raw", [128, 2, F])
        B1A = sb("b1_all", [128, E + 1, FC])
        B2A = sb("b2_all", [128, D])
        WR = sb("wr", [128, E])
        BR = sb("br", [128, E])
        GAM = sb("gamma_bc", [128, D])
        BET = sb("beta_bc", [128, D])
        WQ = sb("wq", [128, D])
        WK = sb("wk", [128, D])
        WV = sb("wv", [128, 2, D // 2])
        WO = sb("wo", [128, D])
        WOZ = sb("wo_half", [128, 2, D])
        ident = sb("ident", [128, 128])
        identb = sb("ident_bf", [128, 128], BF16)
        cmask = sb("causal_mask", [128, 8, S], BF16)
        grp8 = sb("group_of_8", [128, 16])
        grp16 = sb("group_of_16", [128, 8])
        jmask = sb("mask_j", [128, 4])
        r2mask = sb("mask_r2", [128, 2])
        minus_half = sb("minus_half", [128, 4])
        eps = sb("eps", [128, 4])
        ones = sb("ones", [128, 128])
        before = sb("before", [128, 128])
        iota_e = sb("iota_e", [128, E])
        iota_s = sb("iota_slot", [128, SLOTS])
        iota_f = sb("iota_slot_of_block", [128, SLOTS])
        IOT = sb("iota_int", [128, SLOTS], I32)
        bcol = sb("batch_minus_filler", [128, 2])
        CT = sb("ctxT_pair", [128, 2, 256])
        XN = sb("xn", [128, 2, D])
        XK = sb("xnT_and_kT", [128, 512])
        QR = sb("q_by_row_group", [128, 2, 4, 4, S])
        KM = sb("k_by_head", [128, 2, 4, 4, S])
        VM = sb("v_blocks", [128, 2, 4, 8, 2, HD])
        SS = sb("scores_shifted", [128, 2, 512])
        PP = sb("probs", [128, 4, 512])
        PT = sb("probsT", [128, 2, 512])
        AT = sb("attnT", [128, 2, 2, 128])
        MX = sb("row_max", [128, 2, 8])
        SM = sb("row_sum", [128, 2, 8])
        RC = sb("row_sum_recip", [128, 2, 8])
        ST1 = sb("ln1_stats", [128, 2, 6])
        MV1 = sb("ln1_mv", [128, 2, 2])
        RS1 = sb("ln1_rstd", [128, 2])
        SH1 = sb("ln1_shift", [128, 2])
        ST2 = sb("ln2_stats", [128, 2, 6])
        MV2 = sb("ln2_mv", [128, 4, 2])
        RS2 = sb("ln2_rstd", [128, 2])
        SH2 = sb("ln2_shift", [128, 2])
        ZZ = sb("z_pair", [128, 2, D])
        ZS = sb("z_sums", [128, NB])
        RL = sb("router", [128, 12, E])
        RV = sb("router_cols", [128, 17])
        CWT = sb("combine_T", [E, 128 + 24])
        NE1 = sb("expert_counts", [E, 4])
        NEI = sb("expert_counts_int", [E, 2], I32)
        NEB = sb("expert_blocks_bc", [E, 128])
        STI = sb("block_starts_int", [128, E + 1], I32)
        IDX = sb("slot_batch_int", [1, SLOTS], I32)
        OH = PP[:, 2:4, 0:SLOTS]
        OHF = PP[:, 1, 0:SLOTS]
        CW = sb("slot_weight", [128, SLOTS])
        XR = PP[:, 0:1, :].rearrange("p a (h t) -> p (a h) t", h=2)
        XGH = sb("gather_hi", [128, 2, HALF], F32R)
        XGL = sb("gather_lo", [128, 2, HALF], F32R)
        W1H = sb("w1_hi", [128, 2, F], F32R)
        W1L = sb("w1_lo", [128, 2, F], F32R)
        W2H = sb("w2_hi", [128, 2, F], F32R)
        W2L = sb("w2_lo", [128, 2, F], F32R)
        B1E = sb("b1_expert", [128, 2, FC])
        G = QR[:, :, :, :, :].rearrange("p a b c d -> p (a b c d)").rearrange("p (h c t) -> p h c t", h=2, c=FC)
        GH = sb("gelu_hi", [128, 2, FC, HALF], F32R)
        GL = sb("gelu_lo", [128, 2, FC, HALF], F32R)
        ST3 = sb("ln3_stats", [128, 4, 4, 6])
        MV3 = sb("ln3_mv", [128, 4, 4, 2])
        RS3 = sb("ln3_rstd", [128, 4, 4])
        NB3 = sb("ln3_shift", [128, 4, 4])
        YN = KM[:, :, :, :, :].rearrange("p a b c d -> p (a b c d)").rearrange("p (k m d) -> p k m d", k=4, m=4)
        CWX = [SS[:, 0, :], SS[:, 1, :], PT[:, 0, :], PT[:, 1, :]]

        bank = [es.enter_context(nc.psum_tensor(f"bank{n}", [128, 512], F32)) for n in range(8)]
        S_ps, T_ps, A_ps, J0, J1 = bank[0:2], bank[2:4], bank[4:6], bank[6], bank[7]

        d_w, d_x, d_late = sem("d_weights"), sem("d_x"), sem("d_late")
        d_out = [sem(f"d_out{k}") for k in range(4)]
        d_ex = [sem("d_experts_even"), sem("d_experts_odd")]
        d_ct = [sem("d_ctx_even"), sem("d_ctx_odd")]
        g_const, g_chain, v_setup, v_chain = sem("g_const"), sem("g_chain"), sem("v_setup"), sem("v_chain")
        p_s, v_max, v_sub, a_exp = sem("p_scores"), sem("v_max"), sem("v_shifted"), sem("a_exp")
        v_sum, v_rcp, g_norm = sem("v_sum"), sem("v_rcp"), sem("g_norm")
        p_t, a_pt, p_pv = sem("p_probsT"), sem("a_probsT"), sem("p_pv")
        a_at, p_w, v_x2, v_bn1, v_mv1, v_bn2, v_mv2 = (sem("a_attnT"), sem("p_wo"), sem("v_x2"), sem("v_bn1"),
                                                       sem("v_mv1"), sem("v_bn2"), sem("v_mv2"))
        g_eps1, g_rs1, v_sh1, a_xn, p_xk, a_xk, p_q, a_q = (sem("g_eps1"), sem("g_rstd1"), sem("v_shift1"),
                                                            sem("a_xn"), sem("p_xk"), sem("a_xk"), sem("p_q"),
                                                            sem("a_q"))
        g_km, p_v, a_v = sem("g_km"), sem("p_v"), sem("a_v")
        a_qp, g_kmb, a_vh, a_xnp, a_zp = (sem("a_q_part"), sem("g_km_part"), sem("a_v_part"), sem("a_xn_part"),
                                          sem("a_z_part"))
        g_eps2, g_rs2, v_sh2, a_z, p_zt, a_zt, v_zs, g_xb = (sem("g_eps2"), sem("g_rstd2"), sem("v_shift2"),
                                                             sem("a_z"), sem("p_zT"), sem("a_zT"), sem("v_zsum"),
                                                             sem("g_x_plus_beta"))
        p_r, v_r, a_r, v_rt, a_yt = sem("p_route"), sem("v_route"), sem("a_route"), sem("v_top_two"), sem("a_yT")
        d_xr = [sem("d_gather_half0"), sem("d_gather_half1")]
        g_xr = sem("g_gather_last")
        a_hi, g_lo = sem("a_gather_hi"), sem("g_gather_lo")
        a_whi, g_w0, v_w, v_b1 = (sem("a_weights_hi"), sem("g_weights_0_split"), sem("v_weights_split"),
                                  sem("v_b1_expert"))
        v_wl = sem("v_weights_lo_part")
        p_begun = sem("p_expert_begun")
        p_h, a_g, a_gh, v_gh, v_gl, g_gl, p_o, v_c = (sem("p_hidden"), sem("a_gelu"), sem("a_gelu_hi"),
                                                      sem("v_gelu_hi"), sem("v_gelu_lo"), sem("g_gelu_lo"),
                                                      sem("p_ffn_out"), sem("v_combined"))
        p_y, v_bn3, v_mv3, g_eps3, g_rs3, v_nb3 = (sem("p_y"), sem("v_bn3"), sem("v_mv3"), sem("g_eps3"),
                                                   sem("g_rstd3"), sem("v_shift3"))
        v_bn3p, v_mv3p, a_ynp = sem("v_bn3_part"), sem("v_mv3_part"), sem("a_y_normed_part")
        v_gam, v_outp = sem("v_gamma"), sem("v_out_part")
        a_cw = sem("a_token_weights")
        a_yn, g_gam, v_out = sem("a_y_normed"), sem("g_gamma"), sem("v_out")

        block = es.enter_context(nc.Block())

        def load_values(engine, cells, least, most, unchecked=None):
            return nc.values_load_multi_w_load_instructions(cells, engines=(engine,), min_val=least, max_val=most,
                                                            skip_runtime_bounds_check_because=unchecked)[1]

        def expert_bounds(engine, e2):
            return load_values(engine, STI[0:1, bass.ds(2 * e2, 3)], 0, MAXBLK)

        def half_batches(engine, g, half):
            return load_values(engine, IDX[0:1, bass.ds(8 * g + 4 * half, 4)], 0, NB + GB - 1,
                               "a batch or filler by the one-hots")

        def hidden_bank(half, c):
            return bank[c if half == 0 else (4, 5, 0, 1)[c]]

        @block.sync
        def _(sp):
            def load_expert(w1e, w2e, par):
                sp.dma_start(W1R[:, par, :], w1e).then_inc(d_ex[par], 16)
                sp.dma_start(W2R[:, par, :].rearrange("p (c d) -> p c d", d=D),
                             w2e.rearrange("(c p) d -> p c d", p=128)).then_inc(d_ex[par], 16)

            def gather(g):
                for half in range(2):
                    b = half_batches(mybir.EngineType.SP, g, half)
                    sp.wait_ge(g_lo, 2 * g + (half + 1))
                    for k in range(3):
                        sp.dma_start(XR[:, half, S * k:S * k + S],
                                     ZT[:, bass.ds(b[k] * S, S)]).then_inc(d_xr[half], 16)

            def gather_experts(e2, more):
                bounds = expert_bounds(mybir.EngineType.SP, e2)
                for par in range(2):
                    with sp.Fori(bounds[par], bounds[par + 1]) as g:
                        gather(g)
                    if not more and par == 0:
                        sp.wait_ge(v_w, E - 1)
                        load_expert(w1[0], w2[0], 0)
                    elif more:
                        settle(sp, v_setup)
                        sp.wait_ge(v_w, 2 * e2 + (par + 1))
                        load_expert(w1[bass.ds(2 * e2 + (par + 2), 1)].rearrange("o p f -> (o p) f"),
                                    w2[bass.ds(2 * e2 + (par + 2), 1)].rearrange("o f d -> (o f) d"), par)
                return bounds[2]

            xv = x.rearrange("(t p) d -> p t d", p=128)
            sp.dma_start(X[:, 0:4, :], xv[:, 0:4, :]).then_inc(d_x, 16)
            for w_sb, w_dram in ((WQ[:, :], wq), (WK[:, :], wk), (WV[:, :, :], wv), (WO[:, :], wo)):
                sp.dma_start(w_sb, w_dram).then_inc(d_w, 16)
            for p in range(2):
                sp.dma_start(CT[:, p, :], ctxT[:, 256 * p:256 * p + 256]).then_inc(d_ct[p], 16)
            for w_sb, w_dram in ((B1A[:, 0:E, :], b1), (WR[:, :], wr),
                                 (BR[:, :], br.partition_broadcast(128)),
                                 (GAM[:, :], gamma.partition_broadcast(128)),
                                 (BET[:, :], beta.partition_broadcast(128))):
                sp.dma_start(w_sb, w_dram).then_inc(d_late, 16)
            sp.wait_ge(d_x, 16)
            sp.dma_start(X[:, 4:8, :], xv[:, 4:8, :]).then_inc(d_x, 16)
            sp.wait_ge(g_const, 3)
            sp.dma_start(B2A[0:E, :], b2).then_inc(d_late, 16)
            with sp.Fori(1, NP // 2 - 1) as i:
                sp.wait_ge(d_x, 16 * i + 16)
                sp.dma_start(X[:, bass.ds(i * 4 + 4, 4), :], xv[:, bass.ds(i * 4 + 4, 4), :]).then_inc(d_x, 16)
                for par in range(2):
                    sp.wait_ge(p_v, 2 * i + (par - 1))
                    sp.dma_start(CT[:, par, :], ctxT[:, bass.ds(i * 512 + par * 256, 256)]).then_inc(d_ct[par], 16)
            for par in range(2):
                sp.wait_ge(p_v, NP - 3 + par)
                sp.dma_start(CT[:, par, :], ctxT[:, 256 * (NP - 2 + par):256 * (NP - 1 + par)]).then_inc(d_ct[par], 16)
            for e in range(2):
                load_expert(w1[e], w2[e], e)
            sp.wait_ge(v_r, 6)
            sp.wait_ge(g_w0, 2)
            sp.wait_ge(a_zt, NP)
            with sp.Fori(0, E // 2 - 1) as e2:
                gather_experts(e2, True)
            gather(gather_experts(E // 2 - 1, False))
            for k in range(4):
                sp.nop().then_inc(d_out[k], 16)
            ov = out.rearrange("(t p) d -> p t d", p=128)
            with sp.Fori(0, 4) as o:
                for k in range(4):
                    sp.wait_ge(v_out, o * 4 + (k + 1))
                    sp.dma_start(ov[:, bass.ds(o * 16 + 4 * k, 4), :], YN[:, k, :, :]).then_inc(d_out[k], 16)
            for k in range(4):
                sp.wait_ge(d_out[k], 80)

        @block.tensor
        def _(pe):
            def prep_xk(P, par):
                ge(pe, a_xn, P + 1)
                ge(pe, a_q, P)
                for k in range(2):
                    nc.tensor.transpose(J0[:, 128 * k:128 * k + 128], XN[:, k, :], ident[:, :])
                nc.tensor.matmul(J0[:, 256:512], WK[:, :], CT[:, par, :], start=True, stop=True).then_inc(p_xk, 1)

            def prep_q(P):
                ge(pe, a_xk, P + 1)
                nc.tensor.matmul(J0[:, 0:256], WQ[:, :], XK[:, 0:256], start=True, stop=True).then_inc(p_q, 1)

            def prep_v(P, par, x2_before):
                ge(pe, v_x2, x2_before)
                ge(pe, a_v, P)
                for b in range(4):
                    for j2 in range(2):
                        mm = nc.tensor.matmul(J1[64 * j2:64 * j2 + 64, 64 * b:64 * b + 64],
                                              CT[:, par, 64 * b:64 * b + 64], WV[:, j2, :], start=True, stop=True)
                mm.then_inc(p_v, 1)

            def scores(i, k):
                U, P, s, par, ps = 8 * i + k, 2 * i + k // 4, k % 4, k // 4 % 2, S_ps[k % 2]
                if s == 0:
                    ge(pe, a_q, P + 1)
                    ge(pe, g_km, P + 1)
                ge(pe, v_sub, U - 1)
                nc.tensor.matmul(ps[:, :], identb[:, :], cmask[:, :, :].rearrange("p a k -> p (a k)"),
                                 start=True, stop=False, skip_group_check=True)
                for rp in range(2):
                    mm = nc.tensor.matmul(ps[:, 256 * rp:256 * rp + 256],
                                          QR[:, par, s, 2 * rp:2 * rp + 2, :].rearrange("p a k -> p (a k)"),
                                          KM[:, par, s, :, :].rearrange("p a k -> p (a k)"),
                                          start=False, stop=True, skip_group_check=True)
                mm.then_inc(p_s, 1)

            def turn(i, k):
                U = 8 * i + k
                ge(pe, g_norm, U + 1)
                ge(pe, a_pt, U - 1)
                for b in range(4):
                    mm = nc.tensor.transpose(T_ps[k % 2][:, 128 * b:128 * b + 128],
                                             PP[:, k % 4, 128 * b:128 * b + 128], ident[:, :])
                mm.then_inc(p_t, 1)

            def attend(i, k):
                U, P, T, s, par = 8 * i + k, 2 * i + k // 4, 4 * i + k // 2, k % 4, k // 4 % 2
                if s == 0:
                    ge(pe, a_v, P + 1)
                if s % 2 == 0:
                    ge(pe, a_at, T - 1)
                ge(pe, a_pt, U + 1)
                for b in range(4):
                    mm = nc.tensor.matmul(A_ps[k // 2 % 2][32 * b:32 * b + 32, 128 * (k % 2):128 * (k % 2) + 128],
                                          VM[:, par, s, 2 * b:2 * b + 2, :, :].rearrange("p a b c -> p (a b c)"),
                                          PT[:, k % 2, 128 * b:128 * b + 128], start=True, stop=True)
                mm.then_inc(p_pv, 1)

            def project(T, t, z_before, v_before):
                ge(pe, a_at, T + 1)
                ge(pe, v_x2, T)
                ge(pe, a_zt, z_before)
                ge(pe, a_v, v_before)
                for b in range(2):
                    for r2 in range(2):
                        mm = nc.tensor.matmul(J1[64 * b:64 * b + 64, 0:D], AT[:, t, b, 64 * r2:64 * r2 + 64],
                                              WOZ[:, r2, :], start=(r2 == 0), stop=(r2 == 1))
                mm.then_inc(p_w, 1)

            def turn_z(P, x2_before):
                ge(pe, a_z, P + 1)
                ge(pe, v_x2, x2_before)
                if isinstance(P, int):
                    ge(pe, a_zt, P)
                for k in range(2):
                    mm = nc.tensor.transpose(J1[:, 128 * k:128 * k + 128], ZZ[:, k, :], ident[:, :])
                mm.then_inc(p_zt, 1)

            def steps(i):
                static = isinstance(i, int)
                for u in range(8):
                    P, U, s, h = 2 * i + u // 4, 8 * i + u, u % 4, u // 4
                    more = not static or P + 1 < NP
                    if not static or U < NB:
                        scores(i, u)
                    if not static or 0 <= U - 3 < NB:
                        turn(i, u - 3)
                    if not static or 0 <= U - 4 < NB:
                        attend(i, u - 4)
                    if s == 0 and more:
                        pe.wait_ge(d_ct[(h + 1) % 2], 16 * i + 16 * (h + 1))
                        prep_xk(P + 1, (h + 1) % 2)
                    if s == 0 and (not static or 0 <= P - 2 < NP):
                        project(4 * i + (2 * h - 3), 1, P - 3, P + 1 if not static else min(P + 1, NP))
                    if s == 1 and (not static or 0 <= P - 3 < NP):
                        turn_z(P - 3, 4 * i + 2 * h - 2 if not static else min(2 * P - 2, NT))
                    if s == 1 and more:
                        prep_q(P + 1)
                    if s == 2 and (not static or 0 <= P - 1 < NP):
                        project(4 * i + (2 * h - 2), 0, P - 2, P + 1 if not static else min(P + 1, NP))
                    if s == 3 and more:
                        prep_v(P + 1, (h + 1) % 2, 4 * i + 2 * h - 1)

            pe.wait_ge(g_const, 1)
            pe.wait_ge(d_w, 64)
            pe.wait_ge(d_ct[0], 16)
            prep_xk(0, 0)
            prep_q(0)
            prep_v(0, 0, 0)
            pe.wait_ge(g_const, 3)
            pe.wait_ge(v_setup, 4)
            steps(0)
            steps(1)
            with pe.Fori(2, NB // 8 - 1) as i:
                steps(i)
            steps(NB // 8 - 1)
            steps(NB // 8)
            turn_z(NP - 1, NT)

            pe.wait_ge(d_late, 96)
            pe.wait_ge(v_zs, NP)
            pe.wait_ge(a_q, NP)
            nc.tensor.matmul(J0[:, 0:E], ZS[:, :], WR[:, :], start=True, stop=True).then_inc(p_r, 1)
            pe.wait_ge(v_r, 2)
            pe.wait_ge(a_zt, NP)
            nc.tensor.transpose(J1[0:E, 0:128], RL[:, CWR, :], ident[:, :])
            nc.tensor.matmul(A_ps[0][:, 0:E], before[:, :], RL[:, SEL, :], start=True, stop=True)
            nc.tensor.matmul(A_ps[1][0:E, 0:1], RL[:, SEL, :], ones[:, 0:1], start=True, stop=True).then_inc(p_r, 1)
            pe.wait_ge(v_r, 3)
            nc.tensor.matmul(J0[:, 0:E + 1], NEB[:, :], before[0:E, 0:E + 1], start=True, stop=True).then_inc(p_r, 1)
            pe.wait_ge(v_r, 4)
            nc.tensor.matmul(J0[0:1, 0:SLOTS], bcol[:, 0:1], OH[:, 0, :], start=True, stop=False)
            nc.tensor.matmul(J0[0:1, 0:SLOTS], bcol[:, 1:2], OHF, start=False, stop=True).then_inc(p_r, 1)
            pe.wait_ge(v_r, 5)
            nc.tensor.matmul(J1[:, 0:SLOTS], ones[:, :], OH[:, 1, :], start=True, stop=True).then_inc(p_r, 1)

            pe.nop().then_inc(p_h, 8)
            pe.nop().then_inc(p_o, 2)
            pe.wait_ge(v_r, 7)
            pe.wait_ge(g_w0, 2)
            with pe.Fori(0, E // 2) as e2:
                bounds = expert_bounds(mybir.EngineType.PE, e2)
                for par in range(2):
                    pe.wait_ge(v_w, 2 * e2 + (par + 1))
                    pe.nop().then_inc(p_begun, 1)
                    with pe.Fori(bounds[par], bounds[par + 1]) as g:
                        for half in range(2):
                            pe.wait_ge(g_lo, 2 * g + (half + 3))
                            for c in range(FC):
                                last = 8 * g + 4 * half + c + (3 if (half, c) in ((0, 0), (0, 1), (1, 2), (1, 3)) else 1)
                                pe.wait_ge(a_g, last)
                                cols, ps = slice(128 * c, 128 * c + 128), hidden_bank(half, c)[:, 0:HALF]
                                nc.tensor.matmul(ps, W1H[:, par, cols], XGH[:, half, :], start=True, stop=False)
                                nc.tensor.matmul(ps, W1H[:, par, cols], XGL[:, half, :], start=False, stop=False)
                                nc.tensor.matmul(ps, W1L[:, par, cols], XGH[:, half, :],
                                                 start=False, stop=True).then_inc(p_h, 1)
                        for half in range(2):
                            pe.wait_ge(v_c, 8 * g + (4 * half + 4))
                            ps = bank[6 + half][:, 0:HALF]
                            for c in range(FC):
                                pe.wait_ge(g_gl if c < 2 else v_gl, 4 * g + (2 * half + c % 2 + 5))
                                cols = slice(128 * c, 128 * c + 128)
                                nc.tensor.matmul(ps, W2H[:, par, cols], GH[:, half, c, :], start=(c == 0), stop=False)
                                nc.tensor.matmul(ps, W2H[:, par, cols], GL[:, half, c, :], start=False, stop=False)
                                mm = nc.tensor.matmul(ps, W2L[:, par, cols], GH[:, half, c, :],
                                                      start=False, stop=(c == FC - 1))
                            mm.then_inc(p_o, 1)

            blocks = pe.value_load(STI[0:1, E:E + 1], min_val=1, max_val=MAXBLK)
            pe.wait_ge(v_c, 8 * blocks + 8)
            for n in range(NT // 4):
                k = n % 4
                ge(pe, a_yn, n - 3)
                ge(pe, a_cw, n + 1)
                for m in range(4):
                    t, ps = 4 * n + m, bank[k][:, 128 * m:128 * m + 128]
                    nc.tensor.matmul(ps, CWX[k][:, 128 * m:128 * m + 128], B2A[:, :], start=True, stop=False)
                    mm = nc.tensor.matmul(ps, YT[:, 128 * t:128 * t + 128], ident[:, :], start=False, stop=True)
                mm.then_inc(p_y, 1)

        @block.scalar
        def _(act):
            def prep_v(P, par):
                act.wait_ge(p_v, P + 1)
                ge(act, p_pv, 4 * P - 4)
                for j2 in range(2):
                    rows = slice(64 * j2, 64 * j2 + 64)
                    ins = nc.scalar.activation(VM[rows, par, :, :, j2, :].rearrange("p b g d -> p (b g) d"),
                                               J1[rows, 0:256].rearrange("p (n d) -> p n d", d=HD), ACT.Copy)
                    ins.then_inc(a_vh if j2 == 0 else a_v, 1)

            def prep_xk(P):
                act.wait_ge(p_xk, P + 1)
                ge(act, g_km, P)
                ge(act, p_q, P)
                nc.scalar.activation(XK[:, :], J0[:, :], ACT.Copy).then_inc(a_xk, 1)

            def prep_q(P, par):
                act.wait_ge(p_q, P + 1)
                ge(act, p_s, 4 * P - 4)
                for r in range(4):
                    rows = slice(32 * r, 32 * r + 32)
                    nc.scalar.activation(QR[rows, par, :, r, :], J0[rows, 0:256].rearrange("p (b q) -> p b q", q=S),
                                         ACT.Copy).then_inc(a_q if r == 3 else a_qp, 1)

            def norm1(P):
                act.wait_ge(v_sh1, P + 1)
                ge(act, p_xk, P)
                for k in range(2):
                    nc.scalar.activation(XN[:, k, :], X[:, bass.ds(2 * P + k, 1), :].rearrange("p o d -> p (o d)"),
                                         ACT.Identity, bias=SH1[:, k:k + 1],
                                         scale=RS1[:, k:k + 1]).then_inc(a_xnp if k == 0 else a_xn, 1)

            def norm2(P):
                act.wait_ge(v_sh2, P + 1)
                ge(act, p_zt, P)
                for k in range(2):
                    nc.scalar.activation(ZZ[:, k, :], X[:, bass.ds(2 * P + k, 1), :].rearrange("p o d -> p (o d)"),
                                         ACT.Identity, bias=SH2[:, k:k + 1],
                                         scale=RS2[:, k:k + 1]).then_inc(a_zp if k == 0 else a_z, 1)

            def keep_z(P):
                act.wait_ge(p_zt, P + 1)
                nc.scalar.activation(ZT[:, bass.ds(P * 256, 256)], J1[:, 0:256], ACT.Copy).then_inc(a_zt, 1)

            def steps(i):
                static = isinstance(i, int)
                for u in range(8):
                    P, U, s, h = 2 * i + u // 4, 8 * i + u, u % 4, u // 4
                    more = not static or P + 1 < NP
                    if s == 0 and (not static or 1 <= P < NP):
                        prep_v(P, h)
                    if not static or 0 <= U - 1 < NB:
                        act.wait_ge(v_sub, U)
                        ge(act, p_t, U - 4)
                        nc.scalar.activation(PP[:, (u - 1) % 4, :], SS[:, (u - 1) % 2, :], ACT.Exp,
                                             scale=SCALE).then_inc(a_exp, 1)
                    if s == 1 and more:
                        prep_xk(P + 1)
                    if s == 2 and more:
                        prep_q(P + 1, (h + 1) % 2)
                    if not static or 0 <= U - 3 < NB:
                        act.wait_ge(p_t, U - 2)
                        ge(act, p_pv, U - 4)
                        nc.scalar.activation(PT[:, (u - 3) % 2, :], T_ps[(u - 3) % 2][:, :],
                                             ACT.Copy).then_inc(a_pt, 1)
                    if s == 3 and (not static or P + 2 < NP):
                        norm1(P + 2)
                    if s == 0 and (not static or 0 <= P - 3 < NP):
                        norm2(P - 3)
                    if u % 2 == 1 and (not static or 0 <= U - 5 < NB):
                        t = (u - 5) // 2 % 2
                        act.wait_ge(p_pv, U - 3)
                        ge(act, p_w, 4 * i + (u // 2 - 3))
                        nc.scalar.activation(AT[:, t, :, :].rearrange("p b q -> p (b q)"),
                                             A_ps[t][:, 0:256], ACT.Copy).then_inc(a_at, 1)
                    if s == 1 and (not static or 0 <= P - 3 < NP):
                        keep_z(P - 3)

            act.wait_ge(g_const, 1)
            nc.scalar.activation(RV[:, 16:17], eps[:, 0:1], ACT.Exp)
            norm1(0)
            prep_xk(0)
            act.wait_ge(v_setup, 2)
            prep_q(0, 0)
            act.wait_ge(v_setup, 3)
            prep_v(0, 0)
            norm1(1)
            steps(0)
            steps(1)
            with act.Fori(2, NB // 8 - 1) as i:
                steps(i)
            steps(NB // 8 - 1)
            steps(NB // 8)
            norm2(NP - 1)
            keep_z(NP - 1)

            def split_hi(loads, par):
                act.wait_ge(d_ex[par], 32 * loads)
                nc.scalar.activation(W1H[:, par, :], W1R[:, par, :], ACT.Copy).then_inc(a_whi, 1)
                nc.scalar.activation(W2H[:, par, :], W2R[:, par, :], ACT.Copy).then_inc(a_whi, 1)

            act.wait_ge(v_r, 1)
            nc.scalar.activation(RL[:, EXPW, :], RL[:, LOGIT, :], ACT.Exp, bias=RV[:, 1:2]).then_inc(a_r, 1)
            act.wait_ge(v_rt, 1)
            nc.scalar.activation(RV[:, 9:10], RV[:, 8:9], ACT.Exp).then_inc(a_r, 1)
            split_hi(1, 0)
            act.wait_ge(g_const, 6)
            act.wait_ge(a_zt, NP)
            nc.scalar.activation(YT[:, :], ZT[:, :], ACT.Copy).then_inc(a_yt, 1)
            nc.scalar.activation(RV[:, 15:16], RV[:, 8:9], ACT.Gelu)

            act.nop().then_inc(a_g, 8)
            act.wait_ge(v_r, 6)
            def gather_hi(g, half):
                act.wait_ge(d_xr[half], 48 * g + 48)
                act.wait_ge(g_xr, 2 * g + (half + 1))
                act.wait_ge(p_h, 8 * g + (4 * half + 4))
                nc.scalar.activation(XGH[:, half, :], XR[:, half, :], ACT.Copy).then_inc(a_hi, 1)

            for half in range(2):
                gather_hi(0, half)
            with act.Fori(0, E // 2) as e2:
                bounds = expert_bounds(mybir.EngineType.Activation, e2)
                for par in range(2):
                    settle(act, v_setup)
                    act.wait_ge(p_o, 2 * bounds[par] + 2)
                    split_hi(e2 + (par + 1), 1 - par)
                    act.wait_ge(v_b1, 2 * e2 + (par + 1))
                    with act.Fori(bounds[par], bounds[par + 1]) as g:
                        for half in range(2):
                            for c in range(FC):
                                ps, b1e = hidden_bank(half, c)[:, 0:HALF], B1E[:, par, c:c + 1]
                                act.wait_ge(p_h, 8 * g + (4 * half + c + 9))
                                if c == 0:
                                    act.wait_ge(p_o, 2 * g + (half + 1))
                                act.wait_ge(g_gl if c < 2 else v_gl, 4 * g + (2 * half + c % 2 + 1))
                                if c == 0:
                                    nc.scalar.activation(GH[:, half, c, :], ps, ACT.Gelu, bias=b1e).then_inc(a_gh, 1)
                                nc.scalar.activation(G[:, half, c, :], ps, ACT.Gelu, bias=b1e).then_inc(a_g, 1)
                        for half in range(2):
                            gather_hi(g + 1, half)

            def token_weights(n, k):
                nc.scalar.activation(CWX[k][0:E, :].rearrange("p (b q) -> p b q", q=S),
                                     CWT[:, bass.ds(8 * n, 8)].unsqueeze(2).to_broadcast([E, 8, S]),
                                     ACT.Copy).then_inc(a_cw, 1)

            blocks = load_values(mybir.EngineType.Activation, STI[0:1, E:E + 1], 1, MAXBLK)[0]
            act.wait_ge(v_c, 8 * blocks + 8)
            act.wait_ge(g_lo, 2 * blocks + 4)
            for k in range(3):
                token_weights(k, k)
            with act.Fori(0, 4) as o:
                for k in range(4):
                    token_weights(4 * o + (k + 3), (k + 3) % 4)
                    act.wait_ge(v_nb3, 4 * o + (k + 1))
                    act.wait_ge(d_out[k], 16 * o + 16)
                    for m in range(4):
                        nc.scalar.activation(YN[:, k, m, :], bank[k][:, 128 * m:128 * m + 128], ACT.Identity,
                                             bias=NB3[:, k, m:m + 1],
                                             scale=RS3[:, k, m:m + 1]).then_inc(a_yn if m == 3 else a_ynp, 1)

        @block.vector
        def _(dve):
            chain = [0]

            def link(ins):
                chain[0] += 1
                ins.then_inc(v_chain, 1)
                dve.wait_ge(v_chain, chain[0])

            def stats1(P):
                n = 2 * P + 2
                if not isinstance(P, int):
                    dve.wait_ge(v_max, n)
                settle(dve, v_setup)
                ge(dve, v_sh1, P)
                for k in range(2):
                    nc.vector.bn_stats(ST1[:, k, :], X[:, bass.ds(2 * P + k, 1), :].rearrange("p o d -> p (o d)")
                                       ).then_inc(v_bn1, 1)
                settle(dve, v_setup)
                dve.wait_ge(v_bn1, n)
                for k in range(2):
                    nc.vector.bn_aggr(MV1[:, k, :], ST1[:, k, :]).then_inc(v_mv1, 1)

            def shift1(P):
                dve.wait_ge(g_rs1, P + 1)
                nc.vector.scalar_tensor_tensor(SH1[:, :], MV1[:, :, 0], -1.0, RS1[:, :],
                                               ALU.mult, ALU.mult).then_inc(v_sh1, 1)

            def shift2(P, h):
                dve.wait_ge(g_rs2, P + 1)
                nc.vector.scalar_tensor_tensor(SH2[:, :], MV2[:, 2 * h:2 * h + 2, 0], -1.0, RS2[:, :],
                                               ALU.mult, ALU.mult).then_inc(v_sh2, 1)

            def residual(T):
                xt = X[:, bass.ds(T, 1), :].rearrange("p o d -> p (o d)")
                dve.wait_ge(p_w, T + 1)
                nc.vector.tensor_tensor(xt, J1[:, 0:D], xt, ALU.add).then_inc(v_x2, 1)

            def stats2(T, k):
                xt = X[:, bass.ds(T, 1), :].rearrange("p o d -> p (o d)")
                settle(dve, v_setup)
                dve.wait_ge(v_x2, T + 1)
                nc.vector.bn_stats(ST2[:, k, :], xt).then_inc(v_bn2, 1)

            def mean2(T, slot, k):
                settle(dve, v_setup)
                dve.wait_ge(v_bn2, T + 1)
                nc.vector.bn_aggr(MV2[:, slot, :], ST2[:, k, :]).then_inc(v_mv2, 1)

            def zsum(P):
                dve.wait_ge(a_zt, P + 1)
                nc.vector.reduce_sum(ZS[:, bass.ds(4 * P, 4)],
                                     ZT[:, bass.ds(256 * P, 256)].rearrange("p (b q) -> p b q", q=S),
                                     AX.X).then_inc(v_zs, 1)

            def steps(i):
                static = isinstance(i, int)
                for u in range(8):
                    P, U, s, h = 2 * i + u // 4, 8 * i + u, u % 4, u // 4
                    if s == 1:
                        T, slot, k2, late = 4 * i + (2 * h - 3), (2 * h + 1) % 4, 1, not static or 0 <= P - 2 < NP
                    else:
                        T, slot, k2, late = 4 * i + (2 * h - 2), (2 * h - 2) % 4, 0, not static or 0 <= P - 1 < NP
                    late = late and s % 2 == 1
                    before, now, k = not static or 0 <= U - 1 < NB, not static or U < NB, (u - 1) % 8
                    if late:
                        residual(T)
                    if now:
                        ps = S_ps[u % 2][:, :].rearrange("p (n k) -> p n k", k=S)
                        dve.wait_ge(p_s, U + 1)
                        nc.vector.reduce_max(MX[:, u % 2, :], ps, AX.X).then_inc(v_max, 1)
                    if before:
                        dve.wait_ge(a_exp, U)
                        nc.vector.reduce_sum(SM[:, k % 2, :], PP[:, k % 4, :].rearrange("p (n k) -> p n k", k=S),
                                             AX.X).then_inc(v_sum, 1)
                    if late:
                        stats2(T, k2)
                    if now:
                        dve.wait_ge(v_max, U + 1)
                        ge(dve, a_exp, U - 1)
                        nc.vector.tensor_tensor(SS[:, u % 2, :].rearrange("p (n k) -> p n k", k=S), ps,
                                                MX[:, u % 2, :].unsqueeze(2).to_broadcast([128, 8, S]),
                                                ALU.subtract).then_inc(v_sub, 1)
                    if before:
                        dve.wait_ge(v_sum, U)
                        ge(dve, g_norm, U - 2)
                        nc.vector.reciprocal(RC[:, k % 2, :], SM[:, k % 2, :]).then_inc(v_rcp, 1)
                    if late:
                        mean2(T, slot, k2)
                    if s == 0 and (not static or P + 2 < NP):
                        dve.wait_ge(d_x, 16 * i + 32)
                        stats1(P + 2)
                    if s == 2 and (not static or P + 2 < NP):
                        shift1(P + 2)
                    if s == 3 and (not static or 0 <= P - 3 < NP):
                        zsum(P - 3)
                    if s == 3 and (not static or 0 <= P - 2 < NP):
                        shift2(P - 2, h)

            dve.nop().then_inc(v_setup, 1)
            dve.wait_ge(d_x, 16)
            stats1(0)
            nc.vector.memset(QR[:, :, :, :, :], 0.0).then_inc(v_setup, 1)
            shift1(0)
            dve.wait_ge(g_const, 2)
            link(nc.vector.tensor_reduce(jmask[:, :], grp8[:, :].rearrange("p (r j) -> p j r", j=4), AX.X, ALU.add))
            link(nc.vector.tensor_reduce(r2mask[:, :], grp16[:, :].rearrange("p (a b) -> p b a", b=2), AX.X, ALU.add))
            nc.vector.memset(VM[:, :, :, :, :, :], 0.0).then_inc(v_setup, 1)
            dve.wait_ge(d_w, 64)
            link(nc.vector.tensor_scalar(WOZ[:, 0, :], WO[:, :], r2mask[:, 0:1], None, ALU.mult))
            nc.vector.tensor_scalar(WOZ[:, 1, :], WO[:, :], r2mask[:, 1:2], None, ALU.mult).then_inc(v_setup, 1)
            stats1(1)
            shift1(1)
            steps(0)
            steps(1)
            with dve.Fori(2, NB // 8 - 1) as i:
                steps(i)
            steps(NB // 8 - 1)
            steps(NB // 8)
            zsum(NP - 1)

            def pick(w, onehot, top, least):
                link(nc.vector.reduce_max(RV[:, top:top + 1], RL[:, w, :], AX.X))
                link(nc.vector.tensor_scalar(RL[:, TIE, :], RL[:, w, :], RV[:, top:top + 1], None, ALU.is_equal))
                link(nc.vector.scalar_tensor_tensor(RL[:, CAND, :], RL[:, TIE, :], -float(E), iota_e[:, :],
                                                    ALU.mult, ALU.add))
                link(nc.vector.tensor_reduce(RV[:, least:least + 1], RL[:, CAND, :], AX.X, ALU.min))
                link(nc.vector.tensor_scalar(RL[:, onehot, :], RL[:, CAND, :], RV[:, least:least + 1], None,
                                             ALU.is_equal))

            dve.wait_ge(g_const, 4)
            dve.wait_ge(p_r, 1)
            link(nc.vector.scalar_tensor_tensor(RL[:, LOGIT, :], J0[:, 0:E], 1.0 / S, BR[:, :], ALU.mult, ALU.add))
            link(nc.vector.reduce_max(RV[:, 0:1], RL[:, LOGIT, :], AX.X))
            nc.vector.tensor_scalar(RV[:, 1:2], RV[:, 0:1], -1.0, None, ALU.mult).then_inc(v_r, 1)
            dve.wait_ge(a_r, 1)
            link(nc.vector.reduce_sum(RV[:, 2:3], RL[:, EXPW, :], AX.X))
            link(nc.vector.reciprocal(RV[:, 3:4], RV[:, 2:3]))
            link(nc.vector.tensor_scalar(RL[:, PROB, :], RL[:, EXPW, :], RV[:, 3:4], None, ALU.mult))
            pick(PROB, PICK1, 4, 5)
            link(nc.vector.scalar_tensor_tensor(RL[:, REST, :], RL[:, PICK1, :], -4.0, RL[:, PROB, :],
                                                ALU.mult, ALU.add))
            pick(REST, PICK2, 6, 7)
            nc.vector.tensor_tensor(RV[:, 8:9], RV[:, 6:7], RV[:, 4:5], ALU.subtract).then_inc(v_rt, 1)
            dve.wait_ge(a_r, 2)
            link(nc.vector.tensor_scalar(RV[:, 10:11], RV[:, 9:10], 1.0, None, ALU.add))
            link(nc.vector.reciprocal(RV[:, 11:12], RV[:, 10:11]))
            link(nc.vector.tensor_tensor(RV[:, 12:13], RV[:, 9:10], RV[:, 11:12], ALU.mult))
            link(nc.vector.tensor_scalar(RL[:, TIE, :], RL[:, PICK1, :], RV[:, 11:12], None, ALU.mult))
            link(nc.vector.scalar_tensor_tensor(RL[:, CWR, :], RL[:, PICK2, :], RV[:, 12:13], RL[:, TIE, :],
                                                ALU.mult, ALU.add))
            nc.vector.tensor_tensor(RL[:, SEL, :], RL[:, PICK1, :], RL[:, PICK2, :], ALU.add).then_inc(v_r, 1)
            dve.wait_ge(p_r, 2)
            link(nc.vector.tensor_scalar(NEI[:, 0:1], A_ps[1][0:E, 0:1], float(GB - 1), None, ALU.add))
            link(nc.vector.tensor_scalar(NEI[:, 1:2], NEI[:, 0:1], 3, None, ALU.arith_shift_right))
            link(nc.vector.tensor_scalar(NE1[:, 0:1], NEI[:, 1:2], 1.0, None, ALU.max))
            link(nc.vector.tensor_copy(RL[:, POS, :], A_ps[0][:, 0:E]))
            link(nc.vector.tensor_copy(CWT[:, 0:128], J1[0:E, 0:128]))
            nc.vector.tensor_scalar(NEB[:, :], ones[0:E, :], NE1[:, 0:1], None, ALU.mult).then_inc(v_r, 1)
            dve.wait_ge(g_const, 5)
            dve.wait_ge(p_r, 3)
            link(nc.vector.tensor_copy(STI[:, :], J0[:, 0:E + 1]))
            link(nc.vector.scalar_tensor_tensor(RL[:, SLOT, :], J0[:, 0:E], float(GB), RL[:, POS, :],
                                                ALU.mult, ALU.add))
            for n, onehot in enumerate((PICK1, PICK2)):
                link(nc.vector.tensor_tensor(RL[:, TIE, :], RL[:, SLOT, :], RL[:, onehot, :], ALU.mult))
                link(nc.vector.reduce_sum(RV[:, 13 + n:14 + n], RL[:, TIE, :], AX.X))
                link(nc.vector.tensor_scalar(OH[:, n, :], iota_s[:, :], RV[:, 13 + n:14 + n], None, ALU.is_equal))
            link(nc.vector.tensor_scalar(CW[:, :], OH[:, 0, :], RV[:, 11:12], None, ALU.mult))
            link(nc.vector.tensor_tensor(OH[:, 0, :], OH[:, 0, :], OH[:, 1, :], ALU.add))
            nc.vector.tensor_tensor(OHF, OH[:, 0, :], iota_f[:, :], ALU.mult).then_inc(v_r, 1)
            nc.vector.scalar_tensor_tensor(OH[:, 1, :], OH[:, 1, :], RV[:, 12:13], CW[:, :],
                                           ALU.mult, ALU.add).then_inc(v_r, 1)
            dve.wait_ge(p_r, 4)
            nc.vector.scalar_tensor_tensor(IDX[:, :], J0[0:1, 0:SLOTS], float(NOBATCH), iota_f[0:1, :],
                                           ALU.add, ALU.add).then_inc(v_r, 1)
            dve.wait_ge(v_r, 6)
            dve.wait_ge(p_r, 5)
            nc.vector.tensor_copy(CW[:, :], J1[:, 0:SLOTS]).then_inc(v_r, 1)

            dve.nop().then_inc(v_gl, 4)
            dve.nop().then_inc(v_c, 8)
            dve.nop().then_inc(v_w, 1)
            nc.vector.tensor_copy(B1E[:, 0, :], B1A[:, 0, :]).then_inc(v_b1, 1)
            dve.wait_ge(a_yt, 1)
            dve.wait_ge(v_r, 7)
            with dve.Fori(0, E // 2) as e2:
                bounds = expert_bounds(mybir.EngineType.DVE, e2)
                for par in range(2):
                    other = 1 - par
                    dve.wait_ge(a_whi, 4 * e2 + (2 * par + 4))
                    nc.vector.tensor_copy(B1E[:, other, :],
                                          B1A[:, bass.ds(2 * e2 + (par + 1), 1), :].rearrange("p o c -> p (o c)")
                                          ).then_inc(v_b1, 1)
                    nc.vector.tensor_tensor(W1L[:, other, :], W1R[:, other, :], W1H[:, other, :],
                                            ALU.subtract).then_inc(v_wl, 1)
                    nc.vector.tensor_tensor(W2L[:, other, :], W2R[:, other, :], W2H[:, other, :],
                                            ALU.subtract).then_inc(v_w, 1)
                    with dve.Fori(bounds[par], bounds[par + 1]) as g:
                        b = []
                        for half in range(2):
                            dve.wait_ge(p_o, 2 * g + (half + 1))
                            for c in range(1, FC):
                                dve.wait_ge(a_g, 8 * g + (4 * half + c + 9))
                                nc.vector.tensor_copy(GH[:, half, c, :], G[:, half, c, :]).then_inc(v_gh, 1)
                                if c >= 2:
                                    dve.wait_ge(v_gh, 6 * g + (3 * half + c))
                                    nc.vector.tensor_tensor(GL[:, half, c, :], G[:, half, c, :], GH[:, half, c, :],
                                                            ALU.subtract).then_inc(v_gl, 1)
                            b.append(half_batches(mybir.EngineType.DVE, g, half))
                        for half in range(2):
                            dve.wait_ge(p_o, 2 * g + (half + 3))
                            dve.wait_ge(v_c, 8 * g + (4 * half + 8))
                            for k in range(4):
                                yt = YT[:, bass.ds(b[half][k] * S, S)]
                                nc.vector.scalar_tensor_tensor(
                                    yt, bank[6 + half][:, S * k:S * k + S], CW[:, bass.ds(8 * g + (4 * half + k), 1)],
                                    yt, ALU.mult, ALU.add).then_inc(v_c, 1)

            def stats3(o, c):
                k = c % 4
                dve.wait_ge(p_y, 4 * o + (c + 1))
                for m in range(4):
                    nc.vector.bn_stats(ST3[:, k, m, :],
                                       bank[k][:, 128 * m:128 * m + 128]).then_inc(v_bn3 if m == 3 else v_bn3p, 1)
                settle(dve, v_setup)
                dve.wait_ge(v_bn3, 4 * o + (c + 1))
                for m in range(4):
                    nc.vector.bn_aggr(MV3[:, k, m, :], ST3[:, k, m, :]).then_inc(v_mv3 if m == 3 else v_mv3p, 1)

            def shift3(o, c):
                k = c % 4
                dve.wait_ge(g_rs3, 4 * o + (c + 1))
                nc.vector.scalar_tensor_tensor(NB3[:, k, :], MV3[:, k, :, 0], -1.0, RS3[:, k, :],
                                               ALU.mult, ALU.mult).then_inc(v_nb3, 1)

            def finish(o, c):
                k = c % 4
                dve.wait_ge(g_gam, 4 * o + (c + 1))
                yn = YN[:, k, 2:4, :]
                nc.vector.tensor_tensor(yn, yn, GAM[:, :].unsqueeze(1).to_broadcast([128, 2, D]),
                                        ALU.mult).then_inc(v_gam, 1)
                nc.vector.tensor_tensor(YN[:, k, 0:2, :], YN[:, k, 0:2, :], X[:, bass.ds(16 * o + 4 * c, 2), :],
                                        ALU.add).then_inc(v_outp, 1)
                dve.wait_ge(v_gam, 4 * o + (c + 1))
                nc.vector.tensor_tensor(yn, yn, X[:, bass.ds(16 * o + (4 * c + 2), 2), :],
                                        ALU.add).then_inc(v_out, 1)

            dve.wait_ge(g_xb, NP)
            for c in range(4):
                stats3(0, c)
                if c >= 1:
                    shift3(0, c - 1)
                if c >= 2:
                    finish(0, c - 2)
            with dve.Fori(1, 4) as o:
                for c in range(4):
                    stats3(o, c)
                    shift3(o, c - 1)
                    finish(o, c - 2)
            shift3(3, 3)
            finish(3, 2)
            finish(3, 3)

        @block.gpsimd
        def _(pool):
            chain = [0]

            def link(ins):
                chain[0] += 1
                ins.then_inc(g_chain, 1)
                pool.wait_ge(g_chain, chain[0])

            def keep(t, op, base, pattern, mult, fill=0.0):
                link(nc.gpsimd.affine_select(out=t, in_=t, compare_op=op, fill=fill, base=base, pattern=pattern,
                                             channel_multiplier=mult))

            def fill(*pairs):
                for t, v in pairs:
                    chain[0] += 1
                    nc.gpsimd.memset(t, v).then_inc(g_chain, 1)
                pool.wait_ge(g_chain, chain[0])

            fill((eps[:, :], EPS), (minus_half[:, :], -0.5), (ident[:, :], 0.0))
            keep(ident[:, :], ALU.not_equal, 0, [[-1, 128]], 1, 1.0)
            pool.nop().then_inc(g_const, 1)
            fill((grp8[:, :], 1.0), (grp16[:, :], 1.0))
            keep(grp8[:, :], ALU.is_ge, 0, [[-8, 16]], 1)
            keep(grp8[:, :], ALU.is_ge, 7, [[8, 16]], -1)
            keep(grp16[:, :], ALU.is_ge, 0, [[-16, 8]], 1)
            keep(grp16[:, :], ALU.is_ge, 15, [[16, 8]], -1)
            pool.nop().then_inc(g_const, 1)

            def causal_mask():
                fill((cmask[:, :, :], 0.0), (B2A[:, :], 0.0))
                link(nc.gpsimd.tensor_copy(identb[:, :], ident[:, :]))
                for q0 in (0, 64):
                    keep(cmask[q0:q0 + 64, :, :], ALU.is_ge, 0, [[0, 8], [-1, S]], 1, MASKED)
                pool.nop().then_inc(g_const, 1)

            def rstd(mv, rs, eps_sem, rs_sem, n):
                nc.gpsimd.tensor_tensor(rs, mv, eps[:, 0:rs.shape[-1]], ALU.add).then_inc(eps_sem, 1)
                pool.wait_ge(eps_sem, n)
                nc.gpsimd.tensor_tensor(rs, rs, minus_half[:, 0:rs.shape[-1]], ALU.pow).then_inc(rs_sem, 1)

            def rstd1(P):
                pool.wait_ge(v_mv1, 2 * P + 2)
                ge(pool, a_xn, P)
                rstd(MV1[:, :, 1], RS1[:, :], g_eps1, g_rs1, P + 1)

            def rstd2(P, h):
                pool.wait_ge(v_mv2, 2 * P + 2)
                ge(pool, a_z, P)
                rstd(MV2[:, 2 * h:2 * h + 2, 1], RS2[:, :], g_eps2, g_rs2, P + 1)

            def spread_k(P, par, batches):
                pool.wait_ge(a_xk, P + 1)
                ge(pool, p_s, 4 * P - 4)
                for b in batches:
                    ins = nc.gpsimd.tensor_tensor(KM[:, par, b, :, :],
                                                  XK[:, 256 + S * b:256 + S * b + S].unsqueeze(1)
                                                  .to_broadcast([128, 4, S]),
                                                  jmask[:, :].unsqueeze(2).to_broadcast([128, 4, S]), ALU.mult)
                    ins.then_inc(g_km if b == 3 else g_kmb, 1)

            def x_plus_beta(P, tile):
                pool.wait_ge(a_z, P + 1)
                xp = X[:, bass.ds(tile, 2), :]
                nc.gpsimd.tensor_tensor(xp, xp, BET[:, :].unsqueeze(1).to_broadcast([128, 2, D]),
                                        ALU.add).then_inc(g_xb, 1)

            def steps(i):
                static = isinstance(i, int)
                for u in range(8):
                    P, U, s, h = 2 * i + u // 4, 8 * i + u, u % 4, u // 4
                    more = not static or P + 1 < NP
                    if s in (1, 2) and more:
                        spread_k(P + 1, (h + 1) % 2, (2 * s - 2, 2 * s - 1))
                    if not static or 0 <= U - 1 < NB:
                        k = (u - 1) % 8
                        pp = PP[:, k % 4, :].rearrange("p (n k) -> p n k", k=S)
                        pool.wait_ge(v_rcp, U)
                        nc.gpsimd.tensor_tensor(pp, pp, RC[:, k % 2, :].unsqueeze(2).to_broadcast([128, 8, S]),
                                                ALU.mult).then_inc(g_norm, 1)
                    if s == 0 and (not static or 0 <= P - 4 < NP):
                        x_plus_beta(P - 4, 4 * i + (2 * h - 8))
                    if s == 1 and (not static or P + 2 < NP):
                        rstd1(P + 2)
                    if s == 2 and (not static or 0 <= P - 2 < NP):
                        rstd2(P - 2, h)

            rstd1(0)
            causal_mask()
            pool.wait_ge(v_chain, 1)
            spread_k(0, 0, range(4))
            rstd1(1)
            pool.wait_ge(d_late, 96)
            steps(0)
            fill((ones[:, :], 1.0), (before[:, :], 1.0), (bcol[:, 1:2], -1.0))
            keep(before[:, :], ALU.is_gt, 0, [[1, 128]], -1)
            link(nc.gpsimd.iota(IOT[:, 0:1], pattern=[[0, 1]], base=-NOBATCH, channel_multiplier=1))
            link(nc.gpsimd.tensor_copy(bcol[:, 0:1], IOT[:, 0:1]))
            link(nc.gpsimd.iota(IOT[:, :], pattern=[[1, SLOTS]], base=0, channel_multiplier=0))
            link(nc.gpsimd.tensor_copy(iota_e[:, :], IOT[:, 0:E]))
            pool.nop().then_inc(g_const, 1)
            steps(1)
            with pool.Fori(2, NB // 8 - 1) as i:
                steps(i)
            steps(NB // 8 - 1)
            steps(NB // 8)
            x_plus_beta(NP - 2, NT - 4)
            x_plus_beta(NP - 1, NT - 2)
            link(nc.gpsimd.tensor_copy(iota_s[:, :], IOT[:, :]))
            link(nc.gpsimd.iota(IOT[:, :], pattern=[[0, SLOTS // GB], [1, GB]], base=0, channel_multiplier=0))
            link(nc.gpsimd.tensor_copy(iota_f[:, :], IOT[:, :]))
            pool.nop().then_inc(g_const, 1)
            pool.wait_ge(a_pt, NB)
            pool.wait_ge(p_pv, NB)
            for t in (ZT[:, NB * S:], B1A[:, E, :], CWT[:, 128:], SS[:, :, :], PT[:, :, :]):
                link(nc.gpsimd.memset(t, 0.0))
            pool.nop().then_inc(g_const, 1)

            pool.wait_ge(a_whi, 2)
            nc.gpsimd.tensor_tensor(W1L[:, 0, :], W1R[:, 0, :], W1H[:, 0, :], ALU.subtract).then_inc(g_w0, 1)
            nc.gpsimd.tensor_tensor(W2L[:, 0, :], W2R[:, 0, :], W2H[:, 0, :], ALU.subtract).then_inc(g_w0, 1)
            pool.nop().then_inc(g_lo, 2)
            pool.nop().then_inc(g_gl, 4)

            def gather_lo(g, half):
                pool.wait_ge(a_hi, 2 * g + (half + 1))
                nc.gpsimd.tensor_tensor(XGL[:, half, :], XR[:, half, :], XGH[:, half, :],
                                        ALU.subtract).then_inc(g_lo, 1)

            def gather_last(g, half):
                b = pool.value_load(IDX[0:1, bass.ds(8 * g + (4 * half + 3), 1)], min_val=0, max_val=NB + GB - 1)
                nc.gpsimd.tensor_copy(XR[:, half, 3 * S:4 * S], ZT[:, bass.ds(b * S, S)]).then_inc(g_xr, 1)

            pool.wait_ge(v_r, 6)
            pool.wait_ge(a_zt, NP)
            for half in range(2):
                gather_last(0, half)
            for half in range(2):
                gather_lo(0, half)
            blocks = pool.value_load(STI[0:1, E:E + 1], min_val=1, max_val=MAXBLK)
            with pool.Fori(0, blocks) as g:
                for half in range(2):
                    pool.wait_ge(p_o, 2 * g + (half + 1))
                    for c in range(2):
                        if c == 0:
                            pool.wait_ge(a_g, 8 * g + (4 * half + 9))
                        else:
                            pool.wait_ge(v_gh, 6 * g + (3 * half + 1))
                        nc.gpsimd.tensor_tensor(GL[:, half, c, :], G[:, half, c, :], GH[:, half, c, :],
                                                ALU.subtract).then_inc(g_gl, 1)
                    gather_last(g + 1, half)
                for half in range(2):
                    gather_lo(g + 1, half)

            def rstd3(o, c):
                pool.wait_ge(v_mv3, 4 * o + (c + 1))
                rstd(MV3[:, c % 4, :, 1], RS3[:, c % 4, :], g_eps3, g_rs3, 4 * o + (c + 1))

            def scale3(o, c):
                yn = YN[:, c % 4, 0:2, :]
                pool.wait_ge(a_yn, 4 * o + (c + 1))
                nc.gpsimd.tensor_tensor(yn, yn, GAM[:, :].unsqueeze(1).to_broadcast([128, 2, D]),
                                        ALU.mult).then_inc(g_gam, 1)

            for c in range(4):
                rstd3(0, c)
                if c >= 1:
                    scale3(0, c - 1)
            with pool.Fori(1, 4) as o:
                for c in range(4):
                    rstd3(o, c)
                    scale3(o, c - 1)
            scale3(3, 3)


def kernel(**inputs):
    import concourse.bacc as bacc
    from concourse.bass_utils import run_bass_kernel_spmd

    a = {k: np.asarray(v) for k, v in inputs.items()}
    wvT = a["L0_xattn_Wv"].T.reshape(D, 4, 2, 2, HD)
    wv = wvT.transpose(0, 3, 1, 2, 4)
    wv = wv.reshape(D, 2, 2, 2, 2, HD).transpose(0, 1, 2, 4, 3, 5)
    woT = a["L0_xattn_Wo"].T.reshape(2, 2, 2, 2, HD, D)
    arrays = {
        "x": a["x"].reshape(NB * S, D),
        "ctxT": a["ctx_1024"].reshape(NB * S, D).T,
        "wq": a["L0_xattn_Wq"].T,
        "wk": a["L0_xattn_Wk"].T,
        "wv": wv.reshape(D, 2, D // 2),
        "wo": woT.transpose(0, 2, 1, 3, 4, 5).reshape(D, D),
        "w1": a["L0_ffn_W1"],
        "b1": a["L0_ffn_b1"].reshape(E, FC, 128).transpose(2, 0, 1),
        "w2": a["L0_ffn_W2"],
        "b2": a["L0_ffn_b2"],
        "wr": a["L0_ffn_Wr"],
        "br": a["L0_ffn_br"],
        "gamma": a["L0_ffn_gamma"],
        "beta": a["L0_ffn_beta"],
    }
    arrays = {k: np.ascontiguousarray(v) for k, v in arrays.items()}
    nc = bacc.Bacc("TRN2", target_bir_lowering=False, num_devices=1)
    args = {k: nc.dram_tensor("in_" + k, v.shape, F32, kind="ExternalInput").ap() for k, v in arrays.items()}
    out = nc.dram_tensor("out", (NB * S, D), F32, kind="ExternalOutput").ap()
    build(nc, **args, out=out)
    r = run_bass_kernel_spmd(nc, [{"in_" + k: v for k, v in arrays.items()}], core_ids=[0])
    return r.results[0]["out"].reshape(NB, S, D)
```
